# Optimizing a Trainium2 kernel written in Bass

```python
import numpy as np
import jax
import jax.numpy as jnp

def _softmax(x, axis=-1):
    return jax.nn.softmax(x, axis=axis)

def _gelu(x):
    return jax.nn.gelu(x, approximate=True)

def _silu(x):
    return jax.nn.silu(x)

def _sigmoid(x):
    return jax.nn.sigmoid(x)

def _layernorm(x, axis=-1, eps=1e-05):
    m = jnp.mean(x, axis=axis, keepdims=True)
    v = jnp.var(x, axis=axis, keepdims=True)
    return (x - m) / jnp.sqrt(v + eps)

def _scatter_add(tgt, idx, src, axis=0):
    return tgt.at[idx].add(src)

def _segment_sum(src, seg, n):
    return jax.ops.segment_sum(src, seg, n)
kernel_name = 'mk_flamingo_gated_d4_seqx_r8_b4f111'

def setup_inputs(seed: int=0):
    np.random.seed(seed)
    _w = jnp.asarray

    def _rec_inputs():
        import jax
        import jax.numpy as jnp
        _rk = jax.random.key(seed)
        x = -1.394e-06 + 0.9999 * jax.random.normal(jax.random.fold_in(_rk, 1), (16, 128, 128), jnp.float32)
        _lenS = 128 - jax.random.randint(jax.random.fold_in(_rk, 7), (16,), 0, max(1, 128 // 4) + 1, jnp.int32)
        _lenS2 = 128 - jax.random.randint(jax.random.fold_in(_rk, 8), (16,), 0, max(1, 128 // 4) + 1, jnp.int32)
        _ctx_1024P = jax.random.normal(jax.random.fold_in(_rk, 11), (16, 16, 128), jnp.float32)
        _ctx_1024c = jax.random.dirichlet(jax.random.fold_in(_rk, 511), 0.3 * jnp.ones((16,), jnp.float32), (16, 128))
        _ctx_1024t = jnp.einsum('bsk,bkd->bsd', _ctx_1024c, _ctx_1024P)
        _ctx_1024t = _ctx_1024t * jax.lax.rsqrt(jnp.mean(jnp.square(_ctx_1024t)) + 1e-12) * 0.953939
        ctx_1024 = -0.000392918 + 0.999932 * (_ctx_1024t + 0.3 * jax.random.normal(jax.random.fold_in(_rk, 611), (16, 128, 128), jnp.float32))
        _validS = jnp.arange(128)[None, :] < _lenS[:, None]
        _validS2 = jnp.arange(128)[None, :] < _lenS2[:, None]
        _causal = jnp.tril(jnp.ones((128, 128), dtype=bool))
        mask_BxS2_bk0 = jnp.logical_not(jnp.broadcast_to(_validS2[:, :], (16, 128)))
        mask_Bx1xSxS2_ik1 = jnp.where(jnp.broadcast_to(_validS2[:, None, None, :], (16, 1, 128, 128)), 1, 0).astype(jnp.int32)
        mask_Bx1x1xS2_ik0 = jnp.where(jnp.broadcast_to(_validS2[:, None, None, :], (16, 1, 1, 128)), 0, 1).astype(jnp.int32)
        _g = jax.random.normal(jax.random.fold_in(_rk, 9001), (2, 4), jnp.float32)
        _g = jnp.sign(_g) * jnp.maximum(jnp.abs(_g), 1.0) + (_g == 0) * 1.0
        g_xattn = _g[0]
        g_ffn = _g[1]
        return (x, ctx_1024, mask_BxS2_bk0, mask_Bx1xSxS2_ik1, mask_Bx1x1xS2_ik0, g_xattn, g_ffn)
    x, ctx_1024, mask_BxS2_bk0, mask_Bx1xSxS2_ik1, mask_Bx1x1xS2_ik0, g_xattn, g_ffn = _rec_inputs()

    def _L0_xattn_setup():
        import jax, jax.numpy as jnp
        import numpy as np
        DIM = 128
        DIM_LATENT = 128
        DIM_HEAD = 64
        INNER = max(DIM, DIM_LATENT)
        HEADS = INNER // DIM_HEAD
        SCALE = DIM_HEAD ** (-0.5)
        LN_EPS = 1e-05
        RMS_EPS = 1e-08

        def layernorm(x, g, b):
            mu = jnp.mean(x, axis=-1, keepdims=True)
            var = jnp.mean(jnp.square(x - mu), axis=-1, keepdims=True)
            return (x - mu) * jax.lax.rsqrt(var + LN_EPS) * g + b

        def rmsnorm(x, gamma):
            n = jnp.linalg.norm(x, axis=-1, keepdims=True) * x.shape[-1] ** (-0.5)
            return x / jnp.maximum(n, RMS_EPS) * gamma
        key = jax.random.key(seed)
        ks = jax.random.split(key, 8)
        b, n, nl = (8, 256, 64)
        x = jax.random.normal(ks[0], (b, n, DIM), dtype=jnp.float32)
        latents = jax.random.normal(ks[1], (b, nl, DIM_LATENT), dtype=jnp.float32)
        mask = jax.random.randint(ks[2], (b, n), 0, 2).astype(bool)
        init = lambda k, shape, fan_in: jax.random.normal(k, shape, jnp.float32) * fan_in ** (-0.5)
        return {'x': x, 'latents': latents, 'mask': mask, 'ln_x_g': jnp.ones((DIM,), jnp.float32), 'ln_x_b': jnp.zeros((DIM,), jnp.float32), 'ln_l_g': jnp.ones((DIM_LATENT,), jnp.float32), 'ln_l_b': jnp.zeros((DIM_LATENT,), jnp.float32), 'q_gamma': jnp.ones((DIM_HEAD,), jnp.float32), 'k_gamma': jnp.ones((DIM_HEAD,), jnp.float32), 'W_q': init(ks[3], (DIM_LATENT, INNER), DIM_LATENT), 'W_kv': init(ks[4], (DIM, 2 * INNER), DIM), 'W_out': init(ks[5], (INNER, DIM_LATENT), INNER), 'b_out': jnp.zeros((DIM_LATENT,), jnp.float32)}
    _L0_xattn_all = _L0_xattn_setup()
    _L0_xattn_in = {k: v for k, v in _L0_xattn_all.items() if k in ('ln_x_g', 'ln_x_b', 'ln_l_g', 'ln_l_b', 'q_gamma', 'k_gamma', 'W_q', 'W_kv', 'W_out', 'b_out')}
    del _L0_xattn_all

    def _L0_ffn_setup():
        import jax, jax.numpy as jnp
        import numpy as np
        TOP_K = 4
        N_GROUP = 4
        TOPK_GROUP = 2
        ROUTED_SCALING = 2.5

        def _route(x, gate_weight):
            scores = jax.nn.sigmoid(x @ gate_weight.T)
            T, E = scores.shape
            gs = E // N_GROUP
            top2, _ = jax.lax.top_k(scores.reshape(T, N_GROUP, gs), 2)
            group_scores = top2.sum(-1)
            _, gidx = jax.lax.top_k(group_scores, TOPK_GROUP)
            gmask = jax.nn.one_hot(gidx, N_GROUP, dtype=jnp.float32).sum(1)
            smask = jnp.repeat(gmask, gs, axis=1) > 0.5
            masked = jnp.where(smask, scores, 0.0)
            topk_idx = jax.lax.top_k(masked, TOP_K)[1]
            topk_w = jnp.take_along_axis(scores, topk_idx, axis=1)
            topk_w = topk_w / (topk_w.sum(-1, keepdims=True) + 1e-20)
            topk_w = topk_w * ROUTED_SCALING
            combine = jnp.zeros((T, E), jnp.float32).at[jnp.arange(T)[:, None], topk_idx].add(topk_w)
            return combine
        key = jax.random.key(seed)
        ks = jax.random.split(key, 6)
        B, S, H = (2, 128, 128)
        E, I, Is = (16, 64, 256)
        g = lambda k, shape, scale: jax.random.normal(k, shape, dtype=jnp.float32) * scale
        return {'hidden_states': g(ks[0], (B, S, H), 1.0), 'gate_weight': g(ks[1], (E, H), 0.02), 'expert_up': g(ks[2], (E, H, I), 0.02), 'expert_down': g(ks[3], (E, I, H), 0.02), 'shared_up': g(ks[4], (H, Is), 0.02), 'shared_down': g(ks[5], (Is, H), 0.02)}
    _L0_ffn_all = _L0_ffn_setup()
    _L0_ffn_in = {k: v for k, v in _L0_ffn_all.items() if k in ('gate_weight', 'expert_up', 'expert_down', 'shared_up', 'shared_down')}
    del _L0_ffn_all

    def _L1_xattn_setup():
        import jax, jax.numpy as jnp
        import numpy as np
        DIM = 128
        HEADS = 16
        DIM_HEAD = 64
        INNER = HEADS * DIM_HEAD
        SCALE = DIM_HEAD ** (-0.5)
        B, N = (4, 256)

        def _split_heads(t):
            b, n, _ = t.shape
            return t.reshape(b, n, HEADS, DIM_HEAD).transpose(0, 2, 1, 3)

        def _attn_block(q_src, k_src, v_src, Wq, Wk, Wv, Wo, bo):
            q = _split_heads(q_src @ Wq)
            k = _split_heads(k_src @ Wk)
            v = _split_heads(v_src @ Wv)
            dots = jnp.einsum('bhid,bhjd->bhij', q, k) * SCALE
            attn = jax.nn.softmax(dots, axis=-1)
            out = jnp.einsum('bhij,bhjd->bhid', attn, v)
            out = out.transpose(0, 2, 1, 3).reshape(q_src.shape[0], q_src.shape[1], INNER)
            return out @ Wo + bo
        key = jax.random.key(seed)
        ks = jax.random.split(key, 7)
        s = DIM ** (-0.5)
        return {'x1': jax.random.normal(ks[0], (B, N, DIM), jnp.float32), 'x2': jax.random.normal(ks[1], (B, N, DIM), jnp.float32), 'Wq': jax.random.normal(ks[2], (DIM, INNER), jnp.float32) * s, 'Wk': jax.random.normal(ks[3], (DIM, INNER), jnp.float32) * s, 'Wv': jax.random.normal(ks[4], (DIM, INNER), jnp.float32) * s, 'Wo': jax.random.normal(ks[5], (INNER, DIM), jnp.float32) * INNER ** (-0.5), 'bo': jnp.zeros((DIM,), jnp.float32)}
    _L1_xattn_all = _L1_xattn_setup()
    _L1_xattn_in = {k: v for k, v in _L1_xattn_all.items() if k in ('Wq', 'Wk', 'Wv', 'Wo', 'bo')}
    del _L1_xattn_all

    def _L1_ffn_setup():
        import jax, jax.numpy as jnp
        import numpy as np
        BITS = 8
        LORA_RANK = 16
        LORA_ALPHA = 32
        SCALING = LORA_ALPHA / LORA_RANK

        def fake_quant_weight(w, bits=BITS):
            qmax = 2.0 ** (bits - 1) - 1
            scale = jnp.max(jnp.abs(w)) / qmax
            wq = jnp.clip(jnp.round(w / scale), -qmax - 1, qmax) * scale
            return w + jax.lax.stop_gradient(wq - w)

        def qat_lora_linear(x, W, b, A, B):
            Wq = fake_quant_weight(W)
            base = jnp.einsum('bsi,oi->bso', x, Wq) + b
            lora = jnp.einsum('bsr,or->bso', jnp.einsum('bsi,ri->bsr', x, A), B)
            return base + SCALING * lora
        key = jax.random.key(seed)
        ks = jax.random.split(key, 9)
        d, f = (128, 512)
        s_in = 1.0 / np.sqrt(d)
        s_ff = 1.0 / np.sqrt(f)
        return {'hidden_states': jax.random.normal(ks[0], (4, 256, d), jnp.float32), 'W_fc': jax.random.normal(ks[1], (f, d), jnp.float32) * s_in, 'b_fc': jnp.zeros((f,), jnp.float32), 'A_fc': jax.random.normal(ks[2], (LORA_RANK, d), jnp.float32) * s_in, 'B_fc': jnp.zeros((f, LORA_RANK), jnp.float32), 'W_proj': jax.random.normal(ks[3], (d, f), jnp.float32) * s_ff, 'b_proj': jnp.zeros((d,), jnp.float32), 'A_proj': jax.random.normal(ks[4], (LORA_RANK, f), jnp.float32) * s_ff, 'B_proj': jnp.zeros((d, LORA_RANK), jnp.float32)}
    _L1_ffn_all = _L1_ffn_setup()
    _L1_ffn_in = {k: v for k, v in _L1_ffn_all.items() if k in ('W_fc', 'b_fc', 'A_fc', 'B_fc', 'W_proj', 'b_proj', 'A_proj', 'B_proj')}
    del _L1_ffn_all

    def _L2_xattn_setup():
        import jax, jax.numpy as jnp
        import numpy as np
        DIM_MODEL = 128
        NUM_HEADS = 16
        HEAD_DIM = DIM_MODEL // NUM_HEADS
        NEG_INF = -1000000000.0

        def _split_heads(x, B):
            S = x.shape[1]
            return x.reshape(B, S, NUM_HEADS, HEAD_DIM).transpose(0, 2, 1, 3)
        key = jax.random.key(seed)
        ks = jax.random.split(key, 12)
        B, S = (4, 256)
        s = 1.0 / np.sqrt(DIM_MODEL)
        inp = {'query': jax.random.normal(ks[0], (B, S, DIM_MODEL), jnp.float32), 'key': jax.random.normal(ks[1], (B, S, DIM_MODEL), jnp.float32), 'value': jax.random.normal(ks[2], (B, S, DIM_MODEL), jnp.float32), 'mask': jax.random.randint(ks[3], (B, 1, S, S), 0, 2, jnp.int32), 'Wq': jax.random.normal(ks[4], (DIM_MODEL, DIM_MODEL), jnp.float32) * s, 'bq': jnp.zeros((DIM_MODEL,), jnp.float32), 'Wk': jax.random.normal(ks[5], (DIM_MODEL, DIM_MODEL), jnp.float32) * s, 'bk': jnp.zeros((DIM_MODEL,), jnp.float32), 'Wv': jax.random.normal(ks[6], (DIM_MODEL, DIM_MODEL), jnp.float32) * s, 'bv': jnp.zeros((DIM_MODEL,), jnp.float32), 'Wo': jax.random.normal(ks[7], (DIM_MODEL, DIM_MODEL), jnp.float32) * s, 'bo': jnp.zeros((DIM_MODEL,), jnp.float32)}
        return inp
    _L2_xattn_all = _L2_xattn_setup()
    _L2_xattn_in = {k: v for k, v in _L2_xattn_all.items() if k in ('Wq', 'bq', 'Wk', 'bk', 'Wv', 'bv', 'Wo', 'bo')}
    del _L2_xattn_all

    def _L2_ffn_setup():
        import jax, jax.numpy as jnp
        import numpy as np
        HIDDEN = 128
        NUM_EXPERTS = 8
        BATCH, SEQ = (4, 512)
        key = jax.random.key(seed)
        ks = jax.random.split(key, 6)
        s = 1.0 / np.sqrt(HIDDEN)
        tokens = jax.random.normal(ks[0], (BATCH, SEQ, HIDDEN), dtype=jnp.float32)
        gate_w = jax.random.uniform(ks[1], (NUM_EXPERTS, HIDDEN), jnp.float32, -s, s)
        expert_w = jax.random.uniform(ks[2], (NUM_EXPERTS, HIDDEN, HIDDEN), jnp.float32, -s, s)
        expert_b = jax.random.uniform(ks[3], (NUM_EXPERTS, HIDDEN), jnp.float32, -s, s)
        combine_w = jax.random.uniform(ks[4], (HIDDEN, HIDDEN), jnp.float32, -s, s)
        return {'tokens': tokens, 'gate_w': gate_w, 'expert_w': expert_w, 'expert_b': expert_b, 'combine_w': combine_w}
    _L2_ffn_all = _L2_ffn_setup()
    _L2_ffn_in = {k: v for k, v in _L2_ffn_all.items() if k in ('gate_w', 'expert_w', 'expert_b', 'combine_w')}
    del _L2_ffn_all

    def _L3_xattn_setup():
        import jax, jax.numpy as jnp
        import numpy as np
        D_MODEL = 128
        NUM_HEADS = 16
        DEPTH = D_MODEL // NUM_HEADS
        B, S = (2, 256)

        def _split_heads(x):
            b, s, _ = x.shape
            return x.reshape(b, s, NUM_HEADS, DEPTH).transpose(0, 2, 1, 3)
        key = jax.random.key(seed)
        ks = jax.random.split(key, 12)
        std = 1.0 / np.sqrt(D_MODEL)
        inp = {'q': jax.random.normal(ks[0], (B, S, D_MODEL), dtype=jnp.float32), 'k': jax.random.normal(ks[1], (B, S, D_MODEL), dtype=jnp.float32), 'v': jax.random.normal(ks[2], (B, S, D_MODEL), dtype=jnp.float32), 'mask': jax.random.randint(ks[3], (B, 1, 1, S), 0, 2, dtype=jnp.int32), 'wq': jax.random.normal(ks[4], (D_MODEL, D_MODEL), dtype=jnp.float32) * std, 'bq': jnp.zeros((D_MODEL,), dtype=jnp.float32), 'wk': jax.random.normal(ks[5], (D_MODEL, D_MODEL), dtype=jnp.float32) * std, 'bk': jnp.zeros((D_MODEL,), dtype=jnp.float32), 'wv': jax.random.normal(ks[6], (D_MODEL, D_MODEL), dtype=jnp.float32) * std, 'bv': jnp.zeros((D_MODEL,), dtype=jnp.float32), 'wo': jax.random.normal(ks[7], (D_MODEL, D_MODEL), dtype=jnp.float32) * std, 'bo': jnp.zeros((D_MODEL,), dtype=jnp.float32)}
        return inp
    _L3_xattn_all = _L3_xattn_setup()
    _L3_xattn_in = {k: v for k, v in _L3_xattn_all.items() if k in ('wq', 'bq', 'wk', 'bk', 'wv', 'bv', 'wo', 'bo')}
    del _L3_xattn_all

    def _L3_ffn_setup():
        import jax, jax.numpy as jnp
        import numpy as np
        H = 128
        I = 64
        E = 32
        TOP_K = 6
        N_GROUP = 8
        TOPK_GROUP = 4
        SCALE = 2.5
        N_SHARED = 2
        SI = I * N_SHARED
        B, S = (2, 128)
        key = jax.random.key(seed)
        ks = jax.random.split(key, 8)
        x = jax.random.normal(ks[0], (B, S, H), jnp.float32)
        gate_weight = jax.random.normal(ks[1], (E, H), jnp.float32) * 0.02
        e_score_correction_bias = jax.random.normal(ks[2], (E,), jnp.float32) * 0.01
        experts_gate_up = jax.random.normal(ks[3], (E, 2 * I, H), jnp.float32) * 0.02
        experts_down = jax.random.normal(ks[4], (E, H, I), jnp.float32) * 0.02
        shared_gate_w = jax.random.normal(ks[5], (SI, H), jnp.float32) * 0.02
        shared_up_w = jax.random.normal(ks[6], (SI, H), jnp.float32) * 0.02
        shared_down_w = jax.random.normal(ks[7], (H, SI), jnp.float32) * 0.02
        return {'x': x, 'gate_weight': gate_weight, 'e_score_correction_bias': e_score_correction_bias, 'experts_gate_up': experts_gate_up, 'experts_down': experts_down, 'shared_gate_w': shared_gate_w, 'shared_up_w': shared_up_w, 'shared_down_w': shared_down_w}
    _L3_ffn_all = _L3_ffn_setup()
    _L3_ffn_in = {k: v for k, v in _L3_ffn_all.items() if k in ('gate_weight', 'e_score_correction_bias', 'experts_gate_up', 'experts_down', 'shared_gate_w', 'shared_up_w', 'shared_down_w')}
    del _L3_ffn_all
    return {'x': x, 'ctx_1024': ctx_1024, 'mask_BxS2_bk0': mask_BxS2_bk0, 'mask_Bx1xSxS2_ik1': mask_Bx1xSxS2_ik1, 'mask_Bx1x1xS2_ik0': mask_Bx1x1xS2_ik0, 'g_xattn': g_xattn, 'g_ffn': g_ffn, 'L0_xattn_ln_x_g': _L0_xattn_in['ln_x_g'], 'L0_xattn_ln_x_b': _L0_xattn_in['ln_x_b'], 'L0_xattn_ln_l_g': _L0_xattn_in['ln_l_g'], 'L0_xattn_ln_l_b': _L0_xattn_in['ln_l_b'], 'L0_xattn_q_gamma': _L0_xattn_in['q_gamma'], 'L0_xattn_k_gamma': _L0_xattn_in['k_gamma'], 'L0_xattn_W_q': _L0_xattn_in['W_q'], 'L0_xattn_W_kv': _L0_xattn_in['W_kv'], 'L0_xattn_W_out': _L0_xattn_in['W_out'], 'L0_xattn_b_out': _L0_xattn_in['b_out'], 'L0_ffn_gate_weight': _L0_ffn_in['gate_weight'], 'L0_ffn_expert_up': _L0_ffn_in['expert_up'], 'L0_ffn_expert_down': _L0_ffn_in['expert_down'], 'L0_ffn_shared_up': _L0_ffn_in['shared_up'], 'L0_ffn_shared_down': _L0_ffn_in['shared_down'], 'L1_xattn_Wq': _L1_xattn_in['Wq'], 'L1_xattn_Wk': _L1_xattn_in['Wk'], 'L1_xattn_Wv': _L1_xattn_in['Wv'], 'L1_xattn_Wo': _L1_xattn_in['Wo'], 'L1_xattn_bo': _L1_xattn_in['bo'], 'L1_ffn_W_fc': _L1_ffn_in['W_fc'], 'L1_ffn_b_fc': _L1_ffn_in['b_fc'], 'L1_ffn_A_fc': _L1_ffn_in['A_fc'], 'L1_ffn_B_fc': _L1_ffn_in['B_fc'], 'L1_ffn_W_proj': _L1_ffn_in['W_proj'], 'L1_ffn_b_proj': _L1_ffn_in['b_proj'], 'L1_ffn_A_proj': _L1_ffn_in['A_proj'], 'L1_ffn_B_proj': _L1_ffn_in['B_proj'], 'L2_xattn_Wq': _L2_xattn_in['Wq'], 'L2_xattn_bq': _L2_xattn_in['bq'], 'L2_xattn_Wk': _L2_xattn_in['Wk'], 'L2_xattn_bk': _L2_xattn_in['bk'], 'L2_xattn_Wv': _L2_xattn_in['Wv'], 'L2_xattn_bv': _L2_xattn_in['bv'], 'L2_xattn_Wo': _L2_xattn_in['Wo'], 'L2_xattn_bo': _L2_xattn_in['bo'], 'L2_ffn_gate_w': _L2_ffn_in['gate_w'], 'L2_ffn_expert_w': _L2_ffn_in['expert_w'], 'L2_ffn_expert_b': _L2_ffn_in['expert_b'], 'L2_ffn_combine_w': _L2_ffn_in['combine_w'], 'L3_xattn_wq': _L3_xattn_in['wq'], 'L3_xattn_bq': _L3_xattn_in['bq'], 'L3_xattn_wk': _L3_xattn_in['wk'], 'L3_xattn_bk': _L3_xattn_in['bk'], 'L3_xattn_wv': _L3_xattn_in['wv'], 'L3_xattn_bv': _L3_xattn_in['bv'], 'L3_xattn_wo': _L3_xattn_in['wo'], 'L3_xattn_bo': _L3_xattn_in['bo'], 'L3_ffn_gate_weight': _L3_ffn_in['gate_weight'], 'L3_ffn_e_score_correction_bias': _L3_ffn_in['e_score_correction_bias'], 'L3_ffn_experts_gate_up': _L3_ffn_in['experts_gate_up'], 'L3_ffn_experts_down': _L3_ffn_in['experts_down'], 'L3_ffn_shared_gate_w': _L3_ffn_in['shared_gate_w'], 'L3_ffn_shared_up_w': _L3_ffn_in['shared_up_w'], 'L3_ffn_shared_down_w': _L3_ffn_in['shared_down_w']}

def reference(x, ctx_1024, mask_BxS2_bk0, mask_Bx1xSxS2_ik1, mask_Bx1x1xS2_ik0, g_xattn, g_ffn, L0_xattn_ln_x_g, L0_xattn_ln_x_b, L0_xattn_ln_l_g, L0_xattn_ln_l_b, L0_xattn_q_gamma, L0_xattn_k_gamma, L0_xattn_W_q, L0_xattn_W_kv, L0_xattn_W_out, L0_xattn_b_out, L0_ffn_gate_weight, L0_ffn_expert_up, L0_ffn_expert_down, L0_ffn_shared_up, L0_ffn_shared_down, L1_xattn_Wq, L1_xattn_Wk, L1_xattn_Wv, L1_xattn_Wo, L1_xattn_bo, L1_ffn_W_fc, L1_ffn_b_fc, L1_ffn_A_fc, L1_ffn_B_fc, L1_ffn_W_proj, L1_ffn_b_proj, L1_ffn_A_proj, L1_ffn_B_proj, L2_xattn_Wq, L2_xattn_bq, L2_xattn_Wk, L2_xattn_bk, L2_xattn_Wv, L2_xattn_bv, L2_xattn_Wo, L2_xattn_bo, L2_ffn_gate_w, L2_ffn_expert_w, L2_ffn_expert_b, L2_ffn_combine_w, L3_xattn_wq, L3_xattn_bq, L3_xattn_wk, L3_xattn_bk, L3_xattn_wv, L3_xattn_bv, L3_xattn_wo, L3_xattn_bo, L3_ffn_gate_weight, L3_ffn_e_score_correction_bias, L3_ffn_experts_gate_up, L3_ffn_experts_down, L3_ffn_shared_gate_w, L3_ffn_shared_up_w, L3_ffn_shared_down_w):
    import jax
    import jax.numpy as jnp

    def _L0_xattn_ref(x, latents, mask, ln_x_g, ln_x_b, ln_l_g, ln_l_b, q_gamma, k_gamma, W_q, W_kv, W_out, b_out):
        import jax, jax.numpy as jnp
        import numpy as np
        DIM = 128
        DIM_LATENT = 128
        DIM_HEAD = 64
        INNER = max(DIM, DIM_LATENT)
        HEADS = INNER // DIM_HEAD
        SCALE = DIM_HEAD ** (-0.5)
        LN_EPS = 1e-05
        RMS_EPS = 1e-08

        def layernorm(x, g, b):
            mu = jnp.mean(x, axis=-1, keepdims=True)
            var = jnp.mean(jnp.square(x - mu), axis=-1, keepdims=True)
            return (x - mu) * jax.lax.rsqrt(var + LN_EPS) * g + b

        def rmsnorm(x, gamma):
            n = jnp.linalg.norm(x, axis=-1, keepdims=True) * x.shape[-1] ** (-0.5)
            return x / jnp.maximum(n, RMS_EPS) * gamma
        b, n, _ = x.shape
        nl = latents.shape[1]
        xn = layernorm(x, ln_x_g, ln_x_b)
        ln = layernorm(latents, ln_l_g, ln_l_b)
        q = ln @ W_q
        kv = jnp.concatenate([xn @ W_kv, ln @ W_kv], axis=1)
        k, v = (kv[..., :INNER], kv[..., INNER:])
        to_heads = lambda t: t.reshape(t.shape[0], t.shape[1], HEADS, DIM_HEAD).transpose(0, 2, 1, 3)
        q, k, v = (to_heads(q), to_heads(k), to_heads(v))
        qn = rmsnorm(q, q_gamma) * SCALE
        kn = rmsnorm(k, k_gamma)
        sim = jnp.einsum('bhid,bhjd->bhij', qn, kn)
        full_mask = jnp.pad(mask, ((0, 0), (0, nl)), constant_values=True)
        neg = -jnp.finfo(sim.dtype).max
        sim = jnp.where(full_mask[:, None, None, :], sim, neg)
        attn = jax.nn.softmax(sim.astype(jnp.float32), axis=-1).astype(sim.dtype)
        out = jnp.einsum('bhij,bhjd->bhid', attn, v)
        out = out.transpose(0, 2, 1, 3).reshape(b, nl, INNER)
        return out @ W_out + b_out

    def _L0_ffn_ref(hidden_states, gate_weight, expert_up, expert_down, shared_up, shared_down):
        import jax, jax.numpy as jnp
        import numpy as np
        TOP_K = 4
        N_GROUP = 4
        TOPK_GROUP = 2
        ROUTED_SCALING = 2.5

        def _route(x, gate_weight):
            scores = jax.nn.sigmoid(x @ gate_weight.T)
            T, E = scores.shape
            gs = E // N_GROUP
            top2, _ = jax.lax.top_k(scores.reshape(T, N_GROUP, gs), 2)
            group_scores = top2.sum(-1)
            _, gidx = jax.lax.top_k(group_scores, TOPK_GROUP)
            gmask = jax.nn.one_hot(gidx, N_GROUP, dtype=jnp.float32).sum(1)
            smask = jnp.repeat(gmask, gs, axis=1) > 0.5
            masked = jnp.where(smask, scores, 0.0)
            topk_idx = jax.lax.top_k(masked, TOP_K)[1]
            topk_w = jnp.take_along_axis(scores, topk_idx, axis=1)
            topk_w = topk_w / (topk_w.sum(-1, keepdims=True) + 1e-20)
            topk_w = topk_w * ROUTED_SCALING
            combine = jnp.zeros((T, E), jnp.float32).at[jnp.arange(T)[:, None], topk_idx].add(topk_w)
            return combine
        B, S, H = hidden_states.shape
        x = hidden_states.reshape(-1, H)
        combine = _route(x.astype(jnp.float32), gate_weight)
        up = jnp.einsum('th,ehi->eti', x, expert_up)
        down = jnp.einsum('eti,eih->eth', jax.nn.silu(up), expert_down)
        moe_out = jnp.einsum('te,eth->th', combine, down)
        shared = jax.nn.silu(x @ shared_up) @ shared_down
        return (moe_out + shared).reshape(B, S, H)

    def _L1_xattn_ref(x1, x2, Wq, Wk, Wv, Wo, bo):
        import jax, jax.numpy as jnp
        import numpy as np
        DIM = 128
        HEADS = 16
        DIM_HEAD = 64
        INNER = HEADS * DIM_HEAD
        SCALE = DIM_HEAD ** (-0.5)
        B, N = (4, 256)

        def _split_heads(t):
            b, n, _ = t.shape
            return t.reshape(b, n, HEADS, DIM_HEAD).transpose(0, 2, 1, 3)

        def _attn_block(q_src, k_src, v_src, Wq, Wk, Wv, Wo, bo):
            q = _split_heads(q_src @ Wq)
            k = _split_heads(k_src @ Wk)
            v = _split_heads(v_src @ Wv)
            dots = jnp.einsum('bhid,bhjd->bhij', q, k) * SCALE
            attn = jax.nn.softmax(dots, axis=-1)
            out = jnp.einsum('bhij,bhjd->bhid', attn, v)
            out = out.transpose(0, 2, 1, 3).reshape(q_src.shape[0], q_src.shape[1], INNER)
            return out @ Wo + bo
        out = x1 + _attn_block(x1, x2, x2, Wq, Wk, Wv, Wo, bo)
        return _attn_block(out, out, x1, Wq, Wk, Wv, Wo, bo)

    def _L1_ffn_ref(hidden_states, W_fc, b_fc, A_fc, B_fc, W_proj, b_proj, A_proj, B_proj):
        import jax, jax.numpy as jnp
        import numpy as np
        BITS = 8
        LORA_RANK = 16
        LORA_ALPHA = 32
        SCALING = LORA_ALPHA / LORA_RANK

        def fake_quant_weight(w, bits=BITS):
            qmax = 2.0 ** (bits - 1) - 1
            scale = jnp.max(jnp.abs(w)) / qmax
            wq = jnp.clip(jnp.round(w / scale), -qmax - 1, qmax) * scale
            return w + jax.lax.stop_gradient(wq - w)

        def qat_lora_linear(x, W, b, A, B):
            Wq = fake_quant_weight(W)
            base = jnp.einsum('bsi,oi->bso', x, Wq) + b
            lora = jnp.einsum('bsr,or->bso', jnp.einsum('bsi,ri->bsr', x, A), B)
            return base + SCALING * lora
        h = qat_lora_linear(hidden_states, W_fc, b_fc, A_fc, B_fc)
        h = jax.nn.gelu(h, approximate=False)
        h = qat_lora_linear(h, W_proj, b_proj, A_proj, B_proj)
        return h

    def _L2_xattn_ref(query, key, value, mask, Wq, bq, Wk, bk, Wv, bv, Wo, bo):
        import jax, jax.numpy as jnp
        import numpy as np
        DIM_MODEL = 128
        NUM_HEADS = 16
        HEAD_DIM = DIM_MODEL // NUM_HEADS
        NEG_INF = -1000000000.0

        def _split_heads(x, B):
            S = x.shape[1]
            return x.reshape(B, S, NUM_HEADS, HEAD_DIM).transpose(0, 2, 1, 3)
        B = query.shape[0]
        q = _split_heads(query @ Wq + bq, B)
        k = _split_heads(key @ Wk + bk, B)
        v = _split_heads(value @ Wv + bv, B)
        scale = 1.0 / np.sqrt(HEAD_DIM)
        scores = jnp.einsum('bhqd,bhkd->bhqk', q, k) * scale
        scores = jnp.where(mask == 0, NEG_INF, scores)
        probs = jax.nn.softmax(scores, axis=-1)
        attn = jnp.einsum('bhqk,bhkd->bhqd', probs, v)
        attn = attn.transpose(0, 2, 1, 3).reshape(B, -1, DIM_MODEL)
        return attn @ Wo + bo

    def _L2_ffn_ref(tokens, gate_w, expert_w, expert_b, combine_w):
        import jax, jax.numpy as jnp
        import numpy as np
        HIDDEN = 128
        NUM_EXPERTS = 8
        BATCH, SEQ = (4, 512)
        B, S, H = tokens.shape
        logits = jnp.einsum('bsh,eh->bse', tokens, gate_w)
        probs = jax.nn.softmax(logits, axis=-1)
        top2_w, top2_idx = jax.lax.top_k(probs, 2)
        flat = tokens.reshape(B * S, H)
        flat_idx = top2_idx.reshape(B * S, 2)
        flat_w = top2_w.reshape(B * S, 2)
        expert_out = jax.nn.silu(jnp.einsum('nh,edh->ned', flat, expert_w) + expert_b[None, :, :])
        gathered = jnp.take_along_axis(expert_out, flat_idx[:, :, None], axis=1)
        mixed = jnp.sum(gathered * flat_w[:, :, None], axis=1)
        out = jnp.einsum('bsh,dh->bsd', mixed.reshape(B, S, H), combine_w)
        return out

    def _L3_xattn_ref(q, k, v, mask, wq, bq, wk, bk, wv, bv, wo, bo):
        import jax, jax.numpy as jnp
        import numpy as np
        D_MODEL = 128
        NUM_HEADS = 16
        DEPTH = D_MODEL // NUM_HEADS
        B, S = (2, 256)

        def _split_heads(x):
            b, s, _ = x.shape
            return x.reshape(b, s, NUM_HEADS, DEPTH).transpose(0, 2, 1, 3)
        qh = _split_heads(q @ wq + bq)
        kh = _split_heads(k @ wk + bk)
        vh = _split_heads(v @ wv + bv)
        scale = 1.0 / jnp.sqrt(jnp.float32(DEPTH))
        logits = jnp.einsum('bhqd,bhkd->bhqk', qh, kh) * scale
        logits = logits + mask.astype(logits.dtype) * -1000000000.0
        attn = jax.nn.softmax(logits, axis=-1)
        out = jnp.einsum('bhqk,bhkd->bhqd', attn, vh)
        out = out.transpose(0, 2, 1, 3).reshape(q.shape[0], -1, D_MODEL)
        return out @ wo + bo

    def _L3_ffn_ref(x, gate_weight, e_score_correction_bias, experts_gate_up, experts_down, shared_gate_w, shared_up_w, shared_down_w):
        import jax, jax.numpy as jnp
        import numpy as np
        H = 128
        I = 64
        E = 32
        TOP_K = 6
        N_GROUP = 8
        TOPK_GROUP = 4
        SCALE = 2.5
        N_SHARED = 2
        SI = I * N_SHARED
        B, S = (2, 128)
        b, s, h = x.shape
        xf = x.reshape(-1, h)
        T = xf.shape[0]
        logits = xf.astype(jnp.float32) @ gate_weight.astype(jnp.float32).T
        scores = jax.nn.sigmoid(logits)
        sfc = scores + e_score_correction_bias[None, :]
        gs = E // N_GROUP
        group_scores = sfc.reshape(T, N_GROUP, gs).max(axis=-1)
        _, gidx = jax.lax.top_k(group_scores, TOPK_GROUP)
        gmask = jnp.zeros((T, N_GROUP), bool).at[jnp.arange(T)[:, None], gidx].set(True)
        smask = jnp.repeat(gmask, gs, axis=1)
        masked = jnp.where(smask, sfc, 0.0)
        _, topk_idx = jax.lax.top_k(masked, TOP_K)
        tw = jnp.take_along_axis(scores, topk_idx, axis=1)
        tw = tw / (tw.sum(-1, keepdims=True) + 1e-20)
        tw = (tw * SCALE).astype(xf.dtype)
        combine = jnp.zeros((T, E), xf.dtype).at[jnp.arange(T)[:, None], topk_idx].add(tw)

        def expert_step(acc, inp):
            gu, dn, c = inp
            g = xf @ gu[:I].T
            u = xf @ gu[I:].T
            o = jax.nn.silu(g) * u @ dn.T
            return (acc + c[:, None] * o, None)
        routed, _ = jax.lax.scan(expert_step, jnp.zeros_like(xf), (experts_gate_up, experts_down, combine.T))
        sh = jax.nn.silu(xf @ shared_gate_w.T) * (xf @ shared_up_w.T)
        shared_out = sh @ shared_down_w.T
        return (routed + shared_out).reshape(b, s, h)
    x = x + jnp.tanh(g_xattn[0]) * _L0_xattn_ref(ctx_1024, _layernorm(x, axis=-1), mask_BxS2_bk0, L0_xattn_ln_x_g, L0_xattn_ln_x_b, L0_xattn_ln_l_g, L0_xattn_ln_l_b, L0_xattn_q_gamma, L0_xattn_k_gamma, L0_xattn_W_q, L0_xattn_W_kv, L0_xattn_W_out, L0_xattn_b_out)
    x = x + jnp.tanh(g_ffn[0]) * _L0_ffn_ref(_layernorm(x, axis=-1), L0_ffn_gate_weight, L0_ffn_expert_up, L0_ffn_expert_down, L0_ffn_shared_up, L0_ffn_shared_down)
    x = x + jnp.tanh(g_xattn[1]) * _L1_xattn_ref(_layernorm(x, axis=-1), ctx_1024, L1_xattn_Wq, L1_xattn_Wk, L1_xattn_Wv, L1_xattn_Wo, L1_xattn_bo)
    x = x + jnp.tanh(g_ffn[1]) * _L1_ffn_ref(_layernorm(x, axis=-1), L1_ffn_W_fc, L1_ffn_b_fc, L1_ffn_A_fc, L1_ffn_B_fc, L1_ffn_W_proj, L1_ffn_b_proj, L1_ffn_A_proj, L1_ffn_B_proj)
    x = x + jnp.tanh(g_xattn[2]) * _L2_xattn_ref(_layernorm(x, axis=-1), ctx_1024, ctx_1024, mask_Bx1xSxS2_ik1, L2_xattn_Wq, L2_xattn_bq, L2_xattn_Wk, L2_xattn_bk, L2_xattn_Wv, L2_xattn_bv, L2_xattn_Wo, L2_xattn_bo)
    x = x + jnp.tanh(g_ffn[2]) * _L2_ffn_ref(_layernorm(x, axis=-1), L2_ffn_gate_w, L2_ffn_expert_w, L2_ffn_expert_b, L2_ffn_combine_w)
    x = x + jnp.tanh(g_xattn[3]) * _L3_xattn_ref(_layernorm(x, axis=-1), ctx_1024, ctx_1024, mask_Bx1x1xS2_ik0, L3_xattn_wq, L3_xattn_bq, L3_xattn_wk, L3_xattn_bk, L3_xattn_wv, L3_xattn_bv, L3_xattn_wo, L3_xattn_bo)
    x = x + jnp.tanh(g_ffn[3]) * _L3_ffn_ref(_layernorm(x, axis=-1), L3_ffn_gate_weight, L3_ffn_e_score_correction_bias, L3_ffn_experts_gate_up, L3_ffn_experts_down, L3_ffn_shared_gate_w, L3_ffn_shared_up_w, L3_ffn_shared_down_w)
    return x

_drawn_inputs = setup_inputs


def setup_inputs(seed=0):
    import zlib

    import numpy as np

    out = dict(_drawn_inputs(seed))
    spreads = {'L0_xattn_ln_x_g': (1.0, 0.6),
     'L0_xattn_ln_x_b': (0.0, 0.624),
     'L0_xattn_ln_l_g': (1.0, 0.2),
     'L0_xattn_ln_l_b': (0.0, 0.1),
     'L0_xattn_q_gamma': (1.0, 0.6),
     'L0_xattn_k_gamma': (1.0, 0.2),
     'L0_xattn_b_out': (0.0, 0.1),
     'L1_xattn_bo': (0.0, 0.1),
     'L1_ffn_b_fc': (0.0, 0.1),
     'L1_ffn_B_fc': (0.0, 0.1),
     'L1_ffn_b_proj': (0.0, 0.1),
     'L1_ffn_B_proj': (0.0, 0.1),
     'L2_xattn_bq': (0.0, 0.769),
     'L2_xattn_bk': (0.0, 0.8),
     'L2_xattn_bv': (0.0, 0.1),
     'L2_xattn_bo': (0.0, 0.1),
     'L3_xattn_bq': (0.0, 0.658),
     'L3_xattn_bk': (0.0, 0.8),
     'L3_xattn_bv': (0.0, 0.1),
     'L3_xattn_bo': (0.0, 0.1)}
    factors = {'L0_ffn_gate_weight': 4.194,
     'L0_ffn_expert_up': 3.627,
     'L0_ffn_expert_down': 3.607,
     'L2_ffn_expert_b': 8.0,
     'L3_ffn_gate_weight': 8.0,
     'L3_ffn_e_score_correction_bias': 8.0,
     'L3_ffn_experts_gate_up': 8.0,
     'L3_ffn_experts_down': 8.0,
     'L3_ffn_shared_gate_w': 8.0,
     'L3_ffn_shared_up_w': 8.0,
     'L3_ffn_shared_down_w': 8.0}
    for name, (base, spread) in spreads.items():
        noise = np.random.default_rng([zlib.crc32(name.encode()), seed]).standard_normal(out[name].shape)
        drawn = base * np.exp(spread * noise) if base else spread * noise
        out[name] = jnp.asarray(drawn.astype(out[name].dtype))
    for name, factor in factors.items():
        out[name] = (out[name] * factor).astype(out[name].dtype)
    return out
```

```python
import concourse.bass as bass
from concourse import mybir
from contextlib import ExitStack

F32 = mybir.dt.float32
BF16 = mybir.dt.bfloat16
I32 = mybir.dt.int32
U8 = mybir.dt.uint8
ALU = mybir.AluOpType
ACT = mybir.ActivationFunctionType
AX = mybir.AxisListType

P = 128
NB = 16
T = NB * P
GB = 4
NG = NB // GB
GT = GB * P
LN_EPS = 1e-5
MASKED = -float(2.0 ** 100)
ROUND = 12582912.0

COLS = ["ln_x_g", "ln_x_b", "ln_l_g", "ln_l_b", "q_gamma", "k_gamma", "b_out0", "bo1", "b_proj",
        "bq2", "bk2", "bo2", "bq3", "bk3", "bo3"]
COL = {n: i for i, n in enumerate(COLS)}
C_BFC = len(COLS)
C_EB = C_BFC + 4
NCOL = C_EB + 8
R_G, R_BV2, R_BV3, R_SB = 0, 8, 8 + P, 8 + 2 * P
NROW = R_SB + 32


def peeled(eng, n_outer, per, step, longest_lag):
    first = 1 + -(-longest_lag // per)
    for i in range(first):
        for j in range(per):
            step(i, j)
    with eng.Fori(first, n_outer) as i:
        for j in range(per):
            step(i, j)
    for j in range(longest_lag):
        step(n_outer, j)


def back(i, j, lag, per, n_outer):
    j -= lag
    while j < 0:
        i, j = i - 1, j + per
    if isinstance(i, int) and not 0 <= i < n_outer:
        return None
    return i, j


def wait_count(eng, sem, n):
    if isinstance(n, int) and n <= 0:
        return
    eng.wait_ge(sem, n)


class Kernel:

    def __init__(self, nc, ctx, dram, out):
        self.nc, self.ctx, self.dram, self.out = nc, ctx, dram, out
        self.psum = ctx.enter_context(nc.psum_tensor("psum", [P, 8, 512], F32))
        self.bank = [self.psum[:, i, :] for i in range(8)]
        sb = self.sb
        self.x = sb("x", [P, T])
        self.xnt = sb("xnt", [P, T])
        self.ctx_tok = sb("ctx_tok", [P, T])
        self.ctxt = sb("ctxt", [P, T])
        self.big = [sb(f"big{i}", [P, T]) for i in range(3)]
        self.negb = sb("negb", [P, T])
        self.ident = sb("ident", [P, P])
        self.headmask8 = sb("headmask8", [P, 16])
        self.headmask64 = sb("headmask64", [P, 2])
        self.blockmean = sb("blockmean", [P, P])
        self.cols = sb("cols", [P, NCOL])
        self.rows = sb("rows", [P, NROW])
        self.gate = sb("gate", [P, 8])
        self.gbias = sb("gbias", [P, 8])
        self.mv = sb("mv", [P, NB * 2])
        self.bn = sb("bn", [P, 2 * 6])
        self.x_new = sb("x_new", [P, 2, P])
        self.mv_new = sb("mv_new", [P, 2, 2])
        self.rstd = sb("rstd", [P, 4 * NB])
        self.mask0 = sb("mask0", [P, T], U8)
        self.mask2 = sb("mask2", [P, T], I32)
        self.mask3 = self.mask2
        self.w = {}
        self.sels = sb("sels", [P, 2048], BF16)
        self.combt = sb("combt", [P, T], BF16)
        self.own, self.cleared = [], []
        self.work = sb("work", [P, 13 * 1024])
        self.xn = self.work[:, 0:T]
        self.tail_bias = {0: "b_out0", 2: "bo1", 3: "b_proj", 4: "bo2", 6: "bo3"}

    def sb(self, name, shape, dt=F32):
        return self.ctx.enter_context(self.nc.sbuf_tensor(name, shape, dt))

    def sem(self, name):
        one = self.nc.alloc_semaphore(name)
        self.own.append(one)
        return one

    def stage(self, make, *args, **named):
        self.own = []
        make(self, *args, **named)
        for one in self.own:
            self.nc.gpsimd.sem_clear(one)
        for one in self.cleared:
            self.nc.release_semaphore(one)
        self.cleared = self.own

    def col(self, name):
        return self.cols[:, COL[name]:COL[name] + 1]


class Arena:

    def __init__(self, k):
        self.k, self.at = k, 0

    def take(self, words, pattern=None, **sizes):
        a = self.k.work[:, self.at:self.at + words]
        self.at += words
        assert self.at <= 13 * 1024, self.at
        return a.rearrange(pattern, **sizes) if pattern else a


WEIGHTS = {
    "wq0": 128, "wkv0": 256, "wo0": 128,
    "gate0": 16, "up0": 1024, "down0": 1024, "sup0": 256, "sdown0": 256,
    "wq1": 1024, "wk1": 1024, "wv1": 1024, "wo1": 1024,
    "wfc": 512, "wproj": 512,
    "wq2": 128, "wk2": 128, "wv2": 128, "wo2": 128,
    "gate2": 8, "ew2": 1024, "comb2": 128,
    "wq3": 128, "wk3": 128, "wv3": 128, "wo3": 128,
    "gate3": 32, "g3": 2048, "u3": 2048, "down3": 2048, "sg3": 128, "su3": 128, "sd3": 128,
}
SMALL = {"afc": (16, 128), "bfct": (16, 512), "aproj": (16, 512), "bprojt": (16, 128)}


def load_and_constants(k):
    nc, d = k.nc, k.dram
    k.early = early = k.sem("early_loads")
    k.late = {}
    made, conv, tanh_done = k.sem("consts_made"), k.sem("consts_dve"), k.sem("gates_ready")
    early_loads = [(k.x, "x"), (k.ctx_tok, "ctx"), (k.cols, "cols"), (k.rows, "rows")]
    for n, width in WEIGHTS.items():
        k.w[n] = {"g3": k.ctx_tok, "u3": k.big[1]}.get(n) or k.sb("w_" + n, [P, width])
    for n, shape in SMALL.items():
        k.w[n] = k.sb("w_" + n, list(shape))
    stage = {n: int(n[-1]) if n[-1] in "0123" else 1 for n in [*WEIGHTS, *SMALL]}
    for s in range(4):
        k.late[s] = k.sem(f"weights{s}_loaded")
    k.late_count = {s: 0 for s in range(4)}
    ctxt_loaded = k.ctxt_loaded = k.sem("ctxt_loaded")

    with nc.Block() as block:
        @block.sync
        def _(sp):
            for dst, name in early_loads:
                src = d[name]
                sp.dma_start(dst[:, :], src).then_inc(early, 16)
            sp.dma_start(k.mask0[:, :], d["mask0"].broadcast_to([P, T])).then_inc(k.late[0], 16)
            sp.dma_start(k.ctxt[:, :], d["ctxt"]).then_inc(ctxt_loaded, 16)
            k.late_count[0] += 16
            for s in range(4):
                for n in [*WEIGHTS, *SMALL]:
                    if stage[n] == s and n not in ("g3", "u3"):
                        sp.dma_start(k.w[n][:, :], d[n]).then_inc(k.late[s], 16)
                        k.late_count[s] += 16
            sp.dma_start(k.mask2[:, :], d["mask2"]).then_inc(k.late[2], 16)
            k.late_count[2] += 16

        @block.gpsimd
        def _(pool):
            pool.memset(k.ident[:, :], 0.0).then_inc(made, 1)
            pool.memset(k.headmask8[:, :], 1.0).then_inc(made, 1)
            pool.memset(k.headmask64[:, :], 1.0).then_inc(made, 1)
            pool.memset(k.blockmean[:, :], 1.0 / 64).then_inc(made, 1)
            pool.wait_ge(made, 4)
            pool.affine_select(out=k.ident[:, :], in_=k.ident[:, :], compare_op=ALU.not_equal, fill=1.0,
                               base=0, pattern=[[-1, P]], channel_multiplier=1).then_inc(made, 1)
            for n, (m, width, heads, last) in enumerate([(k.headmask8, 8, 16, None),
                                                         (k.headmask64, 64, 2, None)]):
                pool.affine_select(out=m[:, :], in_=m[:, :], compare_op=ALU.is_ge, fill=0.0,
                                   base=0, pattern=[[-width, heads]], channel_multiplier=1).then_inc(made, 1)
                pool.wait_ge(made, 6 + 2 * n)
                pool.affine_select(out=m[:, :], in_=m[:, :], compare_op=ALU.is_ge, fill=0.0,
                                   base=width - 1, pattern=[[width, heads]],
                                   channel_multiplier=-1).then_inc(made, 1)
            b = k.blockmean[:, :].rearrange("p (h c) -> p h c", h=2)
            pool.affine_select(out=b, in_=b, compare_op=ALU.is_ge, fill=0.0, base=0,
                               pattern=[[-64, 2], [0, 64]], channel_multiplier=1).then_inc(made, 1)
            pool.wait_ge(made, 10)
            pool.affine_select(out=b, in_=b, compare_op=ALU.is_ge, fill=0.0, base=63,
                               pattern=[[64, 2], [0, 64]], channel_multiplier=-1).then_inc(made, 1)

        @block.scalar
        def _(act):
            act.wait_ge(early, 64)
            act.activation(k.gate[:, :], k.rows[:, R_G:R_G + 8], ACT.Tanh).then_inc(tanh_done, 1)

        @block.vector
        def _(dve):
            dve.memset(k.gbias[:, :], 0.0).then_inc(conv, 1)
            dve.wait_ge(tanh_done, 1)
            dve.wait_ge(conv, 1)
            for s, name in k.tail_bias.items():
                dve.tensor_tensor(k.gbias[:, s:s + 1], k.gate[:, s:s + 1], k.col(name), ALU.mult)\
                   .then_inc(conv, 1)
            dve.wait_ge(early, 64)
            dve.tensor_scalar(k.col("q_gamma"), k.col("q_gamma"), 0.125, None, ALU.mult).then_inc(conv, 1)
            for name in ("bq2", "bq3"):
                dve.tensor_scalar(k.col(name), k.col(name), 8.0 ** -0.5, None, ALU.mult).then_inc(conv, 1)


def load_into_free(k, pairs):
    with k.nc.Block() as block:
        @block.sync
        def _(sp):
            sp.wait_ge(k.late[2], k.late_count[2])
            for dst, src in pairs:
                sp.dma_start(dst[:, :], src).then_inc(k.late[3], 16)
                k.late_count[3] += 16


def normalise(k, tag, src, dst, dst_t=None, gain=None, bias=None, stats=False):
    nc = k.nc
    chain, rooted = k.sem(f"{tag}_chain"), k.sem(f"{tag}_std")
    normed, turned, copied = k.sem(f"{tag}_normed"), k.sem(f"{tag}_turned"), k.sem(f"{tag}_copied")
    mv = k.mv[:, :].rearrange("p (b two) -> p b two", two=2)
    var, std, r, t = (k.rstd[:, n * NB:(n + 1) * NB] for n in range(4))
    with nc.Block() as block:
        @block.vector
        def _(dve):
            done = [0]

            def link(ins):
                done[0] += 1
                ins.then_inc(chain, 1)
                dve.wait_ge(chain, done[0])

            if stats:
                for b in range(NB):
                    bn = k.bn[:, 6 * (b % 2):6 * (b % 2) + 6]
                    link(dve.bn_stats(bn, src[:, b * P:(b + 1) * P]))
                    ins = dve.bn_aggr(mv[:, b, :], bn)
                link(ins)
            link(dve.tensor_scalar(var, mv[:, :, 1], LN_EPS, None, ALU.add))
            dve.wait_ge(rooted, 1)
            link(dve.reciprocal(r, std))
            link(dve.tensor_tensor(t, r, r, ALU.mult))
            link(dve.tensor_tensor(t, t, var, ALU.mult))
            link(dve.tensor_scalar(t, t, -0.5, 1.5, ALU.mult, ALU.add))
            link(dve.tensor_tensor(r, r, t, ALU.mult))
            for b in range(NB):
                s = slice(b * P, (b + 1) * P)
                dve.tensor_scalar(dst[:, s], src[:, s], mv[:, b, 0:1], r[:, b:b + 1],
                                  ALU.subtract, ALU.mult).then_inc(normed, 1)

        @block.scalar
        def _(act):
            act.wait_ge(chain, (NB + 1 if stats else 0) + 1)
            act.activation(std, var, ACT.Sqrt).then_inc(rooted, 1)
            if dst_t is not None:
                for g in range(NG):
                    act.wait_ge(turned, g + 1)
                    act.activation(dst_t[:, g * GT:(g + 1) * GT], k.bank[g][:, :], ACT.Identity,
                                   scale=gain if gain is not None else 1.0,
                                   bias=bias if bias is not None else 0.0).then_inc(copied, 1)

        @block.tensor
        def _(pe):
            if dst_t is not None:
                for b in range(NB):
                    pe.wait_ge(normed, b + 1)
                    mm = pe.transpose(k.bank[b // GB][:, (b % GB) * P:(b % GB + 1) * P],
                                      dst[:, b * P:(b + 1) * P], k.ident[:, :])
                    if b % GB == GB - 1:
                        mm.then_inc(turned, 1)


def residual(k, dve, sub, b, psum, added, stated, slot, n):
    xb = k.x[:, bass.ds(b * P, P)]
    if sub == 7:
        dve.tensor_tensor(xb, psum, xb, ALU.add).then_inc(added, 1)
        return
    new, bn, mean_var = k.x_new[:, slot, :], k.bn[:, 6 * slot:6 * slot + 6], k.mv_new[:, slot, :]
    dve.tensor_tensor(new, psum, xb, ALU.add).then_inc(added, 1)
    dve.wait_ge(added, n + 1)
    dve.bn_stats(bn, new).then_inc(stated, 1)
    dve.wait_ge(stated, 2 * n + 1)
    dve.tensor_scalar(xb, new, 1.0, None, ALU.mult)
    dve.bn_aggr(mean_var, bn).then_inc(stated, 1)
    dve.wait_ge(stated, 2 * n + 2)
    dve.tensor_scalar(k.mv[:, bass.ds(b * 2, 2)], mean_var, 1.0, None, ALU.mult)



def l0_queries_keys_values(k, lat_t, ctxn_t, qn, kl, kc, v):
    nc, bank = k.nc, k.bank
    a = Arena(k)
    sq, root, inv = (a.take(2 * GT, "p (n c) -> p n c", n=2) for _ in range(3))
    S = {n: k.sem("l0p_" + n) for n in ("proj", "sq", "ms", "root", "guard", "inv", "out", "v", "vc")}
    wq, wkv = k.w["wq0"], k.w["wkv0"]
    jobs = [(src, w, gamma, dst, g) for src, w, gamma, dst in
            ((lat_t, wq[:, :], "q_gamma", qn), (lat_t, wkv[:, 0:P], "k_gamma", kl),
             (ctxn_t, wkv[:, 0:P], "k_gamma", kc)) for g in range(NG)]
    vjobs = [(src, s, g) for s, src in enumerate((ctxn_t, lat_t)) for g in range(NG)]
    N = len(jobs)

    with nc.Block() as block:
        @block.tensor
        def _(pe):
            pe.wait_ge(k.late[0], k.late_count[0])
            for n in range(N + 1):
                if n < N:
                    src, w, _, _, g = jobs[n]
                    if n >= 2:
                        pe.wait_ge(S["out"], n - 1)
                    pe.matmul(bank[n % 2][:, :], w, src[:, g * GT:(g + 1) * GT], start=True, stop=True)\
                      .then_inc(S["proj"], 1)
                if n < len(vjobs):
                    src, s, g = vjobs[n]
                    if n >= 2:
                        pe.wait_ge(S["vc"], n - 1)
                    for b in range(GB):
                        c = (g * GB + b) * P
                        mm = pe.matmul(bank[4 + n % 2][:, b * P:(b + 1) * P], src[:, c:c + P],
                                       wkv[:, P:2 * P], start=True, stop=True)
                    mm.then_inc(S["v"], 1)
                if n >= 1:
                    m = n - 1
                    pe.wait_ge(S["sq"], m + 1)
                    if m >= 2:
                        pe.wait_ge(S["root"], m - 1)
                    pe.matmul(bank[2 + m % 2][:, :], k.blockmean[:, :], sq[:, m % 2, :],
                              start=True, stop=True).then_inc(S["ms"], 1)

        @block.scalar
        def _(act):
            for n in range(N + 1):
                if n < N:
                    act.wait_ge(S["proj"], n + 1)
                    if n >= 2:
                        act.wait_ge(S["ms"], n - 1)
                    act.activation(sq[:, n % 2, :], bank[n % 2][:, :], ACT.Square).then_inc(S["sq"], 1)
                if n < len(vjobs):
                    act.wait_ge(S["v"], n + 1)
                    _, s, g = vjobs[n]
                    act.activation(v[:, s, g * GT:(g + 1) * GT], bank[4 + n % 2][:, :], ACT.Copy)\
                       .then_inc(S["vc"], 1)
                if n >= 1:
                    m = n - 1
                    act.wait_ge(S["ms"], m + 1)
                    if m >= 2:
                        act.wait_ge(S["guard"], m - 1)
                    act.activation(root[:, m % 2, :], bank[2 + m % 2][:, :], ACT.Sqrt)\
                       .then_inc(S["root"], 1)

        @block.vector
        def _(dve):
            for m in range(N):
                src, w, gamma, dst, g = jobs[m]
                dve.wait_ge(S["root"], m + 1)
                dve.tensor_scalar(inv[:, m % 2, :], root[:, m % 2, :], 1e-8, None, ALU.max)\
                   .then_inc(S["guard"], 1)
                dve.wait_ge(S["guard"], m + 1)
                dve.reciprocal(inv[:, m % 2, :], inv[:, m % 2, :]).then_inc(S["inv"], 1)
                dve.wait_ge(S["inv"], m + 1)
                dve.scalar_tensor_tensor(out=dst[:, g * GT:(g + 1) * GT], in0=bank[m % 2][:, :],
                                         scalar=k.col(gamma), in1=inv[:, m % 2, :],
                                         op0=ALU.mult, op1=ALU.mult).then_inc(S["out"], 1)
            dve.tensor_scalar(k.negb[:, :], k.mask0[:, :], 0.0, MASKED, ALU.is_equal, ALU.mult)\
               .then_inc(S["inv"], 1)


def l0_attention(k, qn, kl, kc, v):
    nc, bank, sub = k.nc, k.bank, 0
    a = Arena(k)
    qm = a.take(2 * 256, "p (n h c) -> p n h c", n=2, h=2)
    prob = a.take(2 * 512, "p (n c) -> p n c", n=2)
    probt = a.take(2 * 512, "p (n c) -> p n c", n=2)
    nmax = a.take(4, "p (n h) -> p n h", n=2)
    rsum = a.take(4, "p (n h) -> p n h", n=2)
    rinv = a.take(2)
    on = a.take(P)
    ot = a.take(P)
    yt = a.take(P)
    S = {n: k.sem("l0a_" + n) for n in
         ("qm", "score", "mask", "max", "exp", "turn", "pt", "pv", "inv", "on", "tail1", "ot",
          "proj", "yt", "tail2", "added", "stated")}
    per = 2

    def num(i, j):
        return i * per + j

    tail = Tail(k, S, sub, num, on, ot, yt, k.w["wo0"], 6)

    with nc.Block() as block:
        @block.tensor
        def _(pe):
            def step(i, j):
                if at := back(i, j, 1, per, NB // per):
                    n, c = num(*at), at[1]
                    pe.wait_ge(S["qm"], (n + 1) * 2)
                    wait_count(pe, S["exp"], (n - 1) * 2)
                    for h in range(2):
                        for half, keys in enumerate((kc, kl)):
                            mm = pe.matmul(bank[c][:, h * 256 + half * P:h * 256 + (half + 1) * P],
                                           qm[:, c, h, :], keys[:, bass.ds(n * P, P)],
                                           start=True, stop=True)
                    mm.then_inc(S["score"], 1)
                if at := back(i, j, 2, per, NB // per):
                    n, c = num(*at), at[1]
                    pe.wait_ge(S["exp"], (n + 1) * 2)
                    wait_count(pe, S["pt"], n - 1)
                    for q in range(4):
                        mm = pe.transpose(bank[2 + c][:, q * P:(q + 1) * P],
                                          prob[:, c, q * P:(q + 1) * P], k.ident[:, :])
                    mm.then_inc(S["turn"], 1)
                if at := back(i, j, 3, per, NB // per):
                    n, c = num(*at), at[1]
                    pe.wait_ge(S["pt"], n + 1)
                    wait_count(pe, S["on"], n)
                    for h in range(2):
                        for half in range(2):
                            q = 2 * h + half
                            mm = pe.matmul(bank[4][:, h * 64:(h + 1) * 64],
                                           probt[:, c, q * P:(q + 1) * P],
                                           v[:, half, bass.ds(n * P + h * 64, 64)],
                                           start=(half == 0), stop=(half == 1))
                    mm.then_inc(S["pv"], 1)
                tail.pe_turn(pe, back(i, j, 4, per, NB // per))
                tail.pe_project(pe, back(i, j, 5, per, NB // per))
                tail.pe_back(pe, back(i, j, 6, per, NB // per))
            peeled(pe, NB // per, per, step, 7)

        @block.scalar
        def _(act):
            def step(i, j):
                if at := back(i, j, 2, per, NB // per):
                    n, c = num(*at), at[1]
                    act.wait_ge(S["turn"], n + 1)
                    wait_count(act, S["pv"], n - 1)
                    act.activation(probt[:, c, :], bank[2 + c][:, :], ACT.Copy).then_inc(S["pt"], 1)
                if at := back(i, j, 1, per, NB // per):
                    n, c = num(*at), at[1]
                    act.wait_ge(S["max"], n + 1)
                    wait_count(act, S["turn"], n - 1)
                    wait_count(act, S["inv"], n - 1)
                    for h in range(2):
                        act.activation(prob[:, c, h * 256:(h + 1) * 256], bank[c][:, h * 256:(h + 1) * 256],
                                       ACT.Exp, bias=nmax[:, c, h:h + 1],
                                       accum_out=rsum[:, c, h:h + 1]).then_inc(S["exp"], 1)
                if at := back(i, j, 0, per, NB // per):
                    n, c = num(*at), at[1]
                    wait_count(act, S["score"], n - 1)
                    for h in range(2):
                        act.activation(qm[:, c, h, :], qn[:, bass.ds(n * P, P)], ACT.Copy,
                                       scale=k.headmask64[:, h:h + 1]).then_inc(S["qm"], 1)
                tail.act_turn(act, back(i, j, 4, per, NB // per))
                tail.act_project(act, back(i, j, 5, per, NB // per))
            peeled(act, NB // per, per, step, 6)

        @block.vector
        def _(dve):
            def step(i, j):
                if at := back(i, j, 1, per, NB // per):
                    n, c = num(*at), at[1]
                    dve.wait_ge(S["score"], n + 1)
                    s = bank[c][:, :].rearrange("p (h w) -> p h w", h=2)
                    dve.tensor_tensor(s[:, :, 0:P], s[:, :, 0:P],
                                      k.negb[:, bass.ds(n * P, P)].unsqueeze(1).broadcast_to([P, 2, P]),
                                      ALU.add).then_inc(S["mask"], 1)
                    dve.wait_ge(S["mask"], n + 1)
                    wait_count(dve, S["exp"], (n - 1) * 2)
                    dve.tensor_reduce(nmax[:, c, :], s, AX.X, ALU.max, negate=True).then_inc(S["max"], 1)
                if at := back(i, j, 3, per, NB // per):
                    n, c = num(*at), at[1]
                    dve.wait_ge(S["exp"], (n + 1) * 2)
                    dve.reciprocal(rinv, rsum[:, c, :]).then_inc(S["inv"], 1)
                    dve.wait_ge(S["inv"], n + 1)
                    dve.wait_ge(S["pv"], n + 1)
                    wait_count(dve, S["tail1"], n)
                    dve.tensor_tensor(on.rearrange("p (h c) -> p h c", h=2),
                                      bank[4][:, 0:P].rearrange("p (h c) -> p h c", h=2),
                                      rinv.unsqueeze(2).broadcast_to([P, 2, 64]), ALU.mult)\
                       .then_inc(S["on"], 1)
                tail.dve_add(dve, back(i, j, 6, per, NB // per))
            peeled(dve, NB // per, per, step, 7)


class Tail:

    def __init__(self, k, S, sub, num, on, ot, yt, wo, proj_bank):
        self.k, self.S, self.sub, self.num = k, S, sub, num
        self.on, self.ot, self.yt, self.wo = on, ot, yt, wo
        self.turned, self.proj, self.back = k.bank[5], k.bank[proj_bank], k.bank[7]

    def pe_turn(self, pe, at):
        if at:
            n, S = self.num(*at), self.S
            pe.wait_ge(S["on"], n + 1)
            wait_count(pe, S["ot"], n)
            if self.proj is self.turned:
                wait_count(pe, S["yt"], n)
            pe.transpose(self.turned[:, 0:P], self.on, self.k.ident[:, :]).then_inc(S["tail1"], 1)

    def act_turn(self, act, at):
        if at:
            n, S = self.num(*at), self.S
            act.wait_ge(S["tail1"], n + 1)
            wait_count(act, S["proj"], n)
            act.activation(self.ot, self.turned[:, 0:P], ACT.Copy).then_inc(S["ot"], 1)

    def pe_project(self, pe, at):
        if at:
            n, S = self.num(*at), self.S
            pe.wait_ge(S["ot"], n + 1)
            wait_count(pe, S["yt"], n)
            pe.matmul(self.proj[:, 0:P], self.wo[:, :], self.ot, start=True, stop=True)\
              .then_inc(S["proj"], 1)

    def act_project(self, act, at):
        if at:
            n, S, sub, k = self.num(*at), self.S, self.sub, self.k
            act.wait_ge(S["proj"], n + 1)
            wait_count(act, S["tail2"], n)
            act.activation(self.yt, self.proj[:, 0:P], ACT.Identity, scale=k.gate[:, sub:sub + 1],
                           bias=k.gbias[:, sub:sub + 1]).then_inc(S["yt"], 1)

    def pe_back(self, pe, at):
        if at:
            n, S = self.num(*at), self.S
            pe.wait_ge(S["yt"], n + 1)
            wait_count(pe, S["added"], n)
            pe.transpose(self.back[:, 0:P], self.yt, self.k.ident[:, :]).then_inc(S["tail2"], 1)

    def dve_add(self, dve, at):
        if at:
            n, S = self.num(*at), self.S
            dve.wait_ge(S["tail2"], n + 1)
            residual(self.k, dve, self.sub, n, self.back[:, 0:P], S["added"], S["stated"], 0, n)



def small_head_attention(k, tag, sub, names, bias_q, bias_k, bv, mask, mask_ops, weights_of):
    nc, bank = k.nc, k.bank
    a = Arena(k)
    qt = a.take(2 * P, "p (n c) -> p n c", n=2)
    kt = a.take(2 * P, "p (n c) -> p n c", n=2)
    cs = a.take(2 * P, "p (n c) -> p n c", n=2)
    km = a.take(2 * T, "p (n h c) -> p n h c", n=2, h=16)
    v = a.take(2 * 144, "p (n h c) -> p n h c", n=2, h=16)
    score = a.take(2 * 512, "p (n h c) -> p n h c", n=2, h=4)
    prob = a.take(2 * 512, "p (n c) -> p n c", n=2)
    probt = a.take(2 * 512, "p (n c) -> p n c", n=2)
    nmax = a.take(8, "p (n h) -> p n h", n=2)
    rinv = a.take(16)
    on = a.take(P)
    ot = a.take(P)
    yt = a.take(P)
    S = {n: k.sem(f"{tag}_" + n) for n in
         ("cs", "projqk", "projv", "proj", "qt", "kt", "v", "km", "score", "mask", "max", "exp", "turn", "pt", "pv",
          "inv", "on", "tail1", "ot", "yt", "tail2", "added", "stated", "setup")}
    wq, wk, wv, wo = (k.w[n] for n in names)
    CH = 4
    per, outer = 2 * CH, NB // 2
    scale = 8.0 ** -0.5

    def seq(i, j):
        return i * 2 + j // CH

    def ends(at):
        return at if at and at[1] % CH == CH - 1 else None

    tail = Tail(k, S, sub, seq, on, ot, yt, wo, 5)

    with nc.Block() as block:
        @block.tensor
        def _(pe):
            pe.wait_ge(k.late[weights_of], k.late_count[weights_of])

            def step(i, j):
                if (at := back(i, j, 0, per, outer)) and at[1] % CH == 0:
                    b, c = seq(*at), at[1] // CH
                    wait_count(pe, S["qt"], b)
                    pe.wait_ge(S["cs"], b + 1)
                    pe.matmul(bank[0][:, 0:P], wq[:, :], k.xnt[:, bass.ds(b * P, P)],
                              start=True, stop=True)
                    pe.matmul(bank[0][:, P:2 * P], wk[:, :], cs[:, c, :], start=True, stop=True)\
                      .then_inc(S["projqk"], 1)
                if (at := back(i, j, 2, per, outer)) and at[1] % CH == 0:
                    b, c = seq(*at), at[1] // CH
                    wait_count(pe, S["v"], b)
                    pe.matmul(bank[6][:, 0:P], cs[:, c, :], wv[:, :], start=True, stop=True)\
                      .then_inc(S["projv"], 1)
                if at := back(i, j, 4, per, outer):
                    n, b, c = at[0] * per + at[1], seq(*at), at[1] % CH
                    if c == 0:
                        pe.wait_ge(S["km"], b + 1)
                        pe.wait_ge(S["qt"], b + 1)
                    wait_count(pe, S["mask"], n - 1)
                    pe.matmul(bank[1 + at[1] % 2][:, :], qt[:, at[1] // CH, :],
                              km[:, at[1] // CH, 4 * c:4 * c + 4, :].rearrange("p h c -> p (h c)"),
                              start=True, stop=True).then_inc(S["score"], 1)
                if at := back(i, j, 5, per, outer):
                    n = at[0] * per + at[1]
                    pe.wait_ge(S["exp"], (n + 1) * 4)
                    wait_count(pe, S["pt"], n)
                    for h in range(4):
                        mm = pe.transpose(bank[3][:, h * P:(h + 1) * P],
                                          prob[:, at[1] % 2, h * P:(h + 1) * P], k.ident[:, :])
                    mm.then_inc(S["turn"], 1)
                if at := back(i, j, 6, per, outer):
                    n, b, c = at[0] * per + at[1], seq(*at), at[1] % CH
                    pe.wait_ge(S["pt"], n + 1)
                    if c == 0:
                        pe.wait_ge(S["v"], b + 1)
                        wait_count(pe, S["on"], b)
                    for h in range(4):
                        hh = 4 * c + h
                        mm = pe.matmul(bank[4][:, hh * 9:(hh + 1) * 9],
                                       probt[:, at[1] % 2, h * P:(h + 1) * P],
                                       v[:, at[1] // CH, hh, :], start=True, stop=True)
                    mm.then_inc(S["pv"], 1)
                tail.pe_turn(pe, ends(back(i, j, 7, per, outer)))
                tail.pe_project(pe, ends(back(i, j, 8, per, outer)))
                tail.pe_back(pe, ends(back(i, j, 9, per, outer)))
            peeled(pe, outer, per, step, 10)

        @block.gpsimd
        def _(pool):
            pool.wait_ge(k.ctxt_loaded, 16)

            def step(i, j):
                if (at := back(i, j, 0, per, outer)) and at[1] % CH == 0:
                    b, c = seq(*at), at[1] // CH
                    wait_count(pool, S["projv"], b - 1)
                    pool.tensor_copy(cs[:, c, :], k.ctxt[:, bass.ds(b * P, P)]).then_inc(S["cs"], 1)
                    pool.wait_ge(S["kt"], b + 1)
                    wait_count(pool, S["score"], (b - 1) * CH)
                    pool.tensor_tensor(km[:, c, :, :], kt[:, c, :].unsqueeze(1).broadcast_to([P, 16, P]),
                                       k.headmask8[:, :].unsqueeze(2).broadcast_to([P, 16, P]),
                                       ALU.mult).then_inc(S["km"], 1)
            peeled(pool, outer, per, step, 0)

        @block.scalar
        def _(act):
            def step(i, j):
                if (at := back(i, j, 0, per, outer)) and at[1] % CH == 0:
                    b, c = seq(*at), at[1] // CH
                    act.wait_ge(S["projqk"], b + 1)
                    wait_count(act, S["km"], b - 1)
                    act.activation(kt[:, c, :], bank[0][:, P:2 * P], ACT.Identity, bias=bias_k)\
                       .then_inc(S["kt"], 1)
                    wait_count(act, S["score"], (b - 1) * CH)
                    act.activation(qt[:, c, :], bank[0][:, 0:P], ACT.Identity, scale=scale, bias=bias_q)\
                       .then_inc(S["qt"], 1)
                if at := back(i, j, 5, per, outer):
                    n = at[0] * per + at[1]
                    act.wait_ge(S["turn"], n + 1)
                    wait_count(act, S["pv"], n - 1)
                    act.activation(probt[:, at[1] % 2, :], bank[3][:, :], ACT.Copy).then_inc(S["pt"], 1)
                if at := back(i, j, 4, per, outer):
                    n, m = at[0] * per + at[1], at[1] % 2
                    act.wait_ge(S["max"], n + 1)
                    wait_count(act, S["turn"], n - 1)
                    for h in range(4):
                        act.activation(prob[:, m, h * P:(h + 1) * P], score[:, m, h, :], ACT.Exp,
                                       bias=nmax[:, m, h:h + 1]).then_inc(S["exp"], 1)
                tail.act_turn(act, ends(back(i, j, 7, per, outer)))
                tail.act_project(act, ends(back(i, j, 8, per, outer)))
            peeled(act, outer, per, step, 9)

        @block.vector
        def _(dve):
            dve.wait_ge(k.late[weights_of], k.late_count[weights_of])
            dve.memset(v[:, :, :, 8:9], 1.0)
            dve.tensor_scalar(k.negb[:, :], mask[:, :], mask_ops[0], mask_ops[1], mask_ops[2],
                              mask_ops[3]).then_inc(S["setup"], 1)
            dve.wait_ge(S["setup"], 1)

            def step(i, j):
                if (at := back(i, j, 2, per, outer)) and at[1] % CH == 0:
                    b, c = seq(*at), at[1] // CH
                    dve.wait_ge(S["projv"], b + 1)
                    wait_count(dve, S["pv"], (b - 1) * CH)
                    dve.tensor_tensor(v[:, c, :, 0:8],
                                      bank[6][:, 0:P].rearrange("p (h c) -> p h c", c=8),
                                      bv.rearrange("p (h c) -> p h c", c=8), ALU.add)\
                       .then_inc(S["v"], 1)
                if at := back(i, j, 4, per, outer):
                    n, b, m = at[0] * per + at[1], seq(*at), at[1] % 2
                    dve.wait_ge(S["score"], n + 1)
                    wait_count(dve, S["exp"], (n - 1) * 4)
                    dve.tensor_tensor(score[:, m, :, :],
                                      bank[1 + m][:, :].rearrange("p (h c) -> p h c", h=4),
                                      k.negb[:, bass.ds(b * P, P)].unsqueeze(1).broadcast_to([P, 4, P]),
                                      ALU.add).then_inc(S["mask"], 1)
                    dve.wait_ge(S["mask"], n + 1)
                    dve.tensor_reduce(nmax[:, m, :], score[:, m, :, :], AX.X, ALU.max, negate=True)\
                       .then_inc(S["max"], 1)
                if at := ends(back(i, j, 6, per, outer)):
                    b = seq(*at)
                    dve.wait_ge(S["pv"], (b + 1) * CH)
                    o = bank[4][:, 0:144].rearrange("p (h c) -> p h c", c=9)
                    dve.reciprocal(rinv.unsqueeze(2), o[:, :, 8:9]).then_inc(S["inv"], 1)
                    dve.wait_ge(S["inv"], b + 1)
                    wait_count(dve, S["tail1"], b)
                    dve.tensor_tensor(on.rearrange("p (h c) -> p h c", c=8), o[:, :, 0:8],
                                      rinv.unsqueeze(2).broadcast_to([P, 16, 8]), ALU.mult)\
                       .then_inc(S["on"], 1)
                tail.dve_add(dve, ends(back(i, j, 9, per, outer)))
            peeled(dve, outer, per, step, 10)



def wide_attention(k, tag, q_src, k_src, v_src, out_t=None):
    nc, bank, sub = k.nc, k.bank, 2
    a = Arena(k)
    vs = a.take(2 * P, "p (n c) -> p n c", n=2)
    qk = a.take(2 * 512, "p (n c) -> p n c", n=2)
    v = a.take(4 * 256, "p (n c) -> p n c", n=4)
    prob = a.take(2 * 512, "p (n h c) -> p n h c", n=2, h=4)
    probt = a.take(2 * 512, "p (n c) -> p n c", n=2)
    ot = a.take(2 * 256, "p (n c) -> p n c", n=2)
    nmax = a.take(8, "p (n h) -> p n h", n=2)
    rsum = a.take(8, "p (n h) -> p n h", n=2)
    rinv = a.take(8, "p (n h) -> p n h", n=2)
    yt = a.take(P)
    S = {n: k.sem(f"{tag}_" + n) for n in
         ("vs", "projqk", "projv", "qk", "v", "score", "max", "exp", "inv", "norm", "turn", "pt",
          "pv", "ot", "out", "done", "yt", "tail", "added", "stated")}
    wq, wk, wv, wo = (k.w[n] for n in ("wq1", "wk1", "wv1", "wo1"))
    CH = 4
    per, outer = 2 * CH, NB // 2

    def seq(i, j):
        return i * 2 + j // CH

    with nc.Block() as block:
        @block.tensor
        def _(pe):
            def step(i, j):
                if at := back(i, j, 0, per, outer):
                    n, b, c = at[0] * per + at[1], seq(*at), at[1] % CH
                    wait_count(pe, S["qk"], n)
                    for t in range(2):
                        w = slice((2 * c + t) * P, (2 * c + t + 1) * P)
                        pe.matmul(bank[0][:, t * P:(t + 1) * P], wq[:, w], q_src[:, bass.ds(b * P, P)],
                                  start=True, stop=True)
                        mm = pe.matmul(bank[0][:, (2 + t) * P:(3 + t) * P], wk[:, w],
                                       k_src[:, bass.ds(b * P, P)], start=True, stop=True)
                    mm.then_inc(S["projqk"], 1)
                    wait_count(pe, S["v"], n)
                    pe.wait_ge(S["vs"], b + 1)
                    pe.matmul(bank[1][:, 0:256], vs[:, at[1] // CH, :], wv[:, c * 256:(c + 1) * 256],
                              start=True, stop=True).then_inc(S["projv"], 1)
                if at := back(i, j, 1, per, outer):
                    n, m = at[0] * per + at[1], at[1] % 2
                    pe.wait_ge(S["qk"], n + 1)
                    wait_count(pe, S["exp"], n * 4)
                    for t in range(2):
                        for half in range(2):
                            r, c = 64 * half, t * P
                            mm = pe.matmul(bank[2 + half][:, c:c + P],
                                           qk[r:r + 64, m, t * P:(t + 1) * P],
                                           qk[r:r + 64, m, (2 + t) * P:(3 + t) * P],
                                           start=True, stop=True)
                    mm.then_inc(S["score"], 1)
                if at := back(i, j, 2, per, outer):
                    n, m = at[0] * per + at[1], at[1] % 2
                    pe.wait_ge(S["norm"], n + 1)
                    wait_count(pe, S["pt"], n)
                    for h in range(4):
                        mm = pe.transpose(bank[4][:, h * P:(h + 1) * P], prob[:, m, h, :],
                                          k.ident[:, :])
                    mm.then_inc(S["turn"], 1)
                if at := back(i, j, 3, per, outer):
                    n, m = at[0] * per + at[1], at[1] % 2
                    pe.wait_ge(S["pt"], n + 1)
                    pe.wait_ge(S["v"], n + 1)
                    wait_count(pe, S["ot"], n)
                    for t in range(2):
                        for half in range(2):
                            h, slot = 2 * t + half, 2 * half + t
                            mm = pe.matmul(bank[6][64 * half:64 * half + 64, t * P:(t + 1) * P],
                                           v[:, at[1] % 4, h * 64:(h + 1) * 64],
                                           probt[:, m, slot * P:(slot + 1) * P], start=True, stop=True)
                    mm.then_inc(S["pv"], 1)
                if at := back(i, j, 4, per, outer):
                    n, b, c, m = at[0] * per + at[1], seq(*at), at[1] % CH, at[1] % 2
                    pe.wait_ge(S["ot"], n + 1)
                    if c == 0:
                        wait_count(pe, S["yt" if out_t is None else "done"], b)
                    for t in range(2):
                        w = slice((2 * c + t) * P, (2 * c + t + 1) * P)
                        mm = pe.matmul(bank[7][:, 0:P], wo[:, w], ot[:, m, t * P:(t + 1) * P],
                                       start=(c == 0 and t == 0), stop=(c == CH - 1 and t == 1))
                    mm.then_inc(S["out"], 1)
                if out_t is None and (at := back(i, j, 5, per, outer)) and at[1] % CH == CH - 1:
                    b = seq(*at)
                    pe.wait_ge(S["yt"], b + 1)
                    wait_count(pe, S["added"], b)
                    pe.transpose(bank[5][:, 0:P], yt, k.ident[:, :]).then_inc(S["tail"], 1)
            peeled(pe, outer, per, step, 6)

        @block.gpsimd
        def _(pool):
            def step(i, j):
                if j % CH == 0:
                    b, c = seq(i, j), j // CH
                    wait_count(pool, S["projv"], (b - 1) * CH)
                    pool.tensor_copy(vs[:, c, :], v_src[:, bass.ds(b * P, P)]).then_inc(S["vs"], 1)
            peeled(pool, outer, per, step, 0)

        @block.scalar
        def _(act):
            def step(i, j):
                if at := back(i, j, 0, per, outer):
                    n = at[0] * per + at[1]
                    act.wait_ge(S["projv"], n + 1)
                    wait_count(act, S["pv"], n - 3)
                    act.activation(v[:, at[1] % 4, :], bank[1][:, 0:256], ACT.Copy).then_inc(S["v"], 1)
                if at := back(i, j, 2, per, outer):
                    n, m = at[0] * per + at[1], at[1] % 2
                    act.wait_ge(S["turn"], n + 1)
                    wait_count(act, S["pv"], n - 1)
                    act.activation(probt[:, m, :], bank[4][:, :], ACT.Copy).then_inc(S["pt"], 1)
                if at := back(i, j, 1, per, outer):
                    n, m = at[0] * per + at[1], at[1] % 2
                    act.wait_ge(S["max"], n + 1)
                    wait_count(act, S["turn"], n - 1)
                    for h in range(4):
                        c = (h % 2) * P
                        act.activation(prob[:, m, h, :], bank[2 + h // 2][:, c:c + P], ACT.Exp,
                                       bias=nmax[:, m, h:h + 1],
                                       accum_out=rsum[:, m, h:h + 1]).then_inc(S["exp"], 1)
                if out_t is None and (at := back(i, j, 4, per, outer)) and at[1] % CH == CH - 1:
                    b = seq(*at)
                    act.wait_ge(S["out"], (b + 1) * CH)
                    wait_count(act, S["tail"], b)
                    act.activation(yt, bank[7][:, 0:P], ACT.Identity, scale=k.gate[:, sub:sub + 1],
                                   bias=k.gbias[:, sub:sub + 1]).then_inc(S["yt"], 1)
            peeled(act, outer, per, step, 5)

        @block.vector
        def _(dve):
            def step(i, j):
                if at := back(i, j, 0, per, outer):
                    n, m = at[0] * per + at[1], at[1] % 2
                    dve.wait_ge(S["projqk"], n + 1)
                    wait_count(dve, S["score"], n - 1)
                    dve.tensor_copy(qk[:, m, :], bank[0][:, :]).then_inc(S["qk"], 1)
                if at := back(i, j, 1, per, outer):
                    n, m = at[0] * per + at[1], at[1] % 2
                    dve.wait_ge(S["score"], n + 1)
                    wait_count(dve, S["exp"], (n - 1) * 4)
                    dve.tensor_reduce(nmax[:, m, :].rearrange("p (half t) -> p half t", half=2),
                                      k.psum[:, 2:4, 0:256]
                                      .rearrange("p half (t c) -> p half t c", t=2),
                                      AX.X, ALU.max, negate=True).then_inc(S["max"], 1)
                if at := back(i, j, 3, per, outer):
                    n, m = at[0] * per + at[1], at[1] % 2
                    dve.wait_ge(S["pv"], n + 1)
                    wait_count(dve, S["out"], n - 1)
                    dve.tensor_copy(ot[:, m, :], bank[6][:, 0:256]).then_inc(S["ot"], 1)
                if at := back(i, j, 1, per, outer):
                    n, m = at[0] * per + at[1], at[1] % 2
                    dve.wait_ge(S["exp"], (n + 1) * 4)
                    dve.reciprocal(rinv[:, m, :], rsum[:, m, :]).then_inc(S["inv"], 1)
                    dve.wait_ge(S["inv"], n + 1)
                    dve.tensor_tensor(prob[:, m, :, :], prob[:, m, :, :],
                                      rinv[:, m, :].unsqueeze(2).broadcast_to([P, 4, P]), ALU.mult)\
                       .then_inc(S["norm"], 1)
                if (at := back(i, j, 4, per, outer)) and at[1] % CH == CH - 1 and out_t is not None:
                    b = seq(*at)
                    dve.wait_ge(S["out"], (b + 1) * CH)
                    dve.scalar_tensor_tensor(out=out_t[:, bass.ds(b * P, P)], in0=bank[7][:, 0:P],
                                             scalar=k.col("bo1"), in1=k.xnt[:, bass.ds(b * P, P)],
                                             op0=ALU.add, op1=ALU.add).then_inc(S["done"], 1)
                if (at := back(i, j, 5, per, outer)) and at[1] % CH == CH - 1 and out_t is None:
                    b = seq(*at)
                    dve.wait_ge(S["tail"], b + 1)
                    residual(k, dve, sub, b, bank[5][:, 0:P], S["added"], S["stated"], 0, b)
            peeled(dve, outer, per, step, 6)



def feed_forward(k, tag, sub, tiles, function):
    nc, bank = k.nc, k.bank
    J = len(tiles)
    a = Arena(k)
    h1 = a.take(2 * GT, "p (n c) -> p n c", n=2)
    h2 = a.take(2 * GT, "p (n c) -> p n c", n=2)
    h3 = a.take(2 * GT, "p (n c) -> p n c", n=2)
    yt = a.take(GT)
    S = {n: k.sem(f"{tag}_" + n) for n in
         ("up", "act", "second", "made_dve", "made_act", "down", "yt", "tail", "added", "stated", "stored")}
    second = tiles[0][2] is not None
    last_sub = sub == 7

    by_dve = [t[2] is not None or t[3] is not None for t in tiles]
    NV = sum(by_dve)

    def free(j):
        return 2 if j >= 2 or J % 2 == 0 else (1, 3)[j]

    def wait_hidden(eng, g, j):
        if by_dve[j]:
            eng.wait_ge(S["made_dve"], g * NV + sum(by_dve[:j + 1]))
        else:
            eng.wait_ge(S["made_act"], g * (J - NV) + j + 1 - sum(by_dve[:j + 1]))

    def wait_last_hidden(eng, at):
        if before := back(*at, free(at[1]), J, NG):
            wait_hidden(eng, *before)

    with nc.Block() as block:
        @block.tensor
        def _(pe):
            def step(i, j):
                if at := back(i, j, 0, J, NG):
                    n, m = at[0] * J + at[1], at[1] % 2
                    up, _, sec, sel, _ = tiles[at[1]]
                    group = bass.ds(at[0] * GT, GT)
                    wait_last_hidden(pe, at)
                    mm = pe.matmul(bank[m][:, :], up, k.xnt[:, group], start=True, stop=True)
                    if sec is not None:
                        mm = pe.matmul(bank[2 + m][:, :], sec, k.xnt[:, group], start=True, stop=True)
                    if sel is not None:
                        mm = pe.matmul(bank[4 + m][:, :], sel, k.combt[:, group], start=True, stop=True)
                    mm.then_inc(S["up"], 1)
                if at := back(i, j, 2, J, NG):
                    n, m = at[0] * J + at[1], at[1] % 2
                    wait_hidden(pe, *at)
                    if at[1] == 0:
                        wait_count(pe, S["yt"], at[0])
                    pe.matmul(bank[6][:, :], tiles[at[1]][4], h3[:, m, :], start=(at[1] == 0),
                              stop=(at[1] == J - 1)).then_inc(S["down"], 1)
                if (at := back(i, j, 3, J, NG)) and at[1] == J - 1:
                    pe.wait_ge(S["yt"], at[0] + 1)
                    wait_count(pe, S["added"], at[0] * (1 if last_sub else GB))
                    for b in range(GB):
                        mm = pe.transpose(bank[7][:, b * P:(b + 1) * P], yt[:, b * P:(b + 1) * P],
                                          k.ident[:, :])
                    mm.then_inc(S["tail"], 1)
            peeled(pe, NG, J, step, 3)

        @block.scalar
        def _(act):
            def step(i, j):
                if (at := back(i, j, 2, J, NG)) and at[1] == J - 1:
                    act.wait_ge(S["down"], (at[0] + 1) * J)
                    wait_count(act, S["tail"], at[0])
                    act.activation(yt, bank[6][:, :], ACT.Identity, scale=k.gate[:, sub:sub + 1],
                                   bias=k.gbias[:, sub:sub + 1]).then_inc(S["yt"], 1)
                if at := back(i, j, 0, J, NG):
                    n, m = at[0] * J + at[1], at[1] % 2
                    _, bias, _, sel, _ = tiles[at[1]]
                    act.wait_ge(S["up"], n + 1)
                    if by_dve[at[1]]:
                        wait_last_hidden(act, at)
                        act.activation(h1[:, m, :], bank[m][:, :], function,
                                       bias=bias if bias is not None else 0.0).then_inc(S["act"], 1)
                    else:
                        wait_count(act, S["down"], n + 1 - free(at[1]))
                        act.activation(h3[:, m, :], bank[m][:, :], function,
                                       bias=bias if bias is not None else 0.0)\
                           .then_inc(S["made_act"], 1)
            peeled(act, NG, J, step, 3)

        @block.vector
        def _(dve):
            experts = sum(t[3] is not None for t in tiles)

            def step(i, j):
                if at := back(i, j, 0, J, NG):
                    g, t = at
                    n, m = g * J + t, t % 2
                    _, _, sec, sel, _ = tiles[t]
                    if by_dve[t]:
                        dve.wait_ge(S["act"], g * NV + sum(by_dve[:t + 1]))
                        wait_count(dve, S["down"], n + 1 - free(t))
                        if second and sel is not None:
                            dve.tensor_tensor(h2[:, m, :], bank[2 + m][:, :], h1[:, m, :], ALU.mult)\
                               .then_inc(S["second"], 1)
                            dve.wait_ge(S["second"], g * experts + t + 1)
                            dve.tensor_tensor(h3[:, m, :], bank[4 + m][:, :], h2[:, m, :], ALU.mult)\
                               .then_inc(S["made_dve"], 1)
                        else:
                            src = bank[4 + m] if sel is not None else bank[2 + m]
                            dve.tensor_tensor(h3[:, m, :], src[:, :], h1[:, m, :], ALU.mult)\
                               .then_inc(S["made_dve"], 1)
                if (at := back(i, j, 3, J, NG)) and at[1] == J - 1:
                    g = at[0]
                    dve.wait_ge(S["tail"], g + 1)
                    if last_sub:
                        xg = k.x[:, bass.ds(g * GT, GT)]
                        dve.tensor_tensor(xg, bank[7][:, :], xg, ALU.add).then_inc(S["added"], 1)
                    else:
                        for b in range(GB):
                            residual(k, dve, sub, g * GB + b, bank[7][:, b * P:(b + 1) * P],
                                     S["added"], S["stated"], b % 2, g * GB + b)
            peeled(dve, NG, J, step, 4 if J >= 4 else 3)

        if last_sub:
            @block.sync
            def _(sp):
                for g in range(NG):
                    sp.wait_ge(S["added"], g + 1)
                    sp.dma_start(k.out[:, g * GT:(g + 1) * GT], k.x[:, g * GT:(g + 1) * GT])\
                      .then_inc(S["stored"], 16)
                sp.wait_ge(S["stored"], 16 * NG)


def make_selectors(pool, k, experts, width, sem, n):
    s = k.sels[:, 0:experts * width].rearrange("p (e c) -> p e c", c=width)
    pool.memset(k.sels[:, 0:experts * width], 0.0).then_inc(sem, 1)
    for part in range(3):
        pool.wait_ge(sem, n + part + 1)
        pool.affine_select(out=s, in_=s, compare_op=ALU.not_equal, fill=1.0, base=-part * experts,
                           pattern=[[-1, experts], [0, width]], channel_multiplier=1).then_inc(sem, 1)


def route(k, tag, E, groups, top_groups, top, kind, gate_w, rbias=None, factor=1.0, width=64,
          weights_of=0):
    nc, bank = k.nc, k.bank
    a = Arena(k)
    st = a.take(T)
    TE = NB * E

    def take():
        return a.take(TE, "p (t e) -> p t e", t=NB)

    s, v, rank, cmp, sel, w = take(), take(), take(), take(), take(), take()
    G = groups or 1
    gs = E // G
    gsc, grank, gcmp = (a.take(NB * G, "p (t g) -> p t g", t=NB) for _ in range(3))
    tmp = [a.take(NB * G, "p (t g) -> p t g", t=NB) for _ in range(4)]
    tot, parts = a.take(NB), a.take(3 * TE, "p (t q e) -> p t q e", t=NB, q=3)
    low = a.take(TE, "p (t e) -> p t e", t=NB)
    bf = k.big[2][:, 0:(TE + 1) // 2].bitcast(BF16).rearrange("p (t e) -> p t e", t=NB)
    S = {n: k.sem(f"{tag}_" + n) for n in
         ("logit", "st", "turn", "chain", "exp", "parts", "turn2", "comb", "sel")}

    with nc.Block() as block:
        @block.tensor
        def _(pe):
            pe.wait_ge(k.late[weights_of], k.late_count[weights_of])
            for g in range(NG):
                pe.matmul(bank[g][0:E, :], gate_w, k.xnt[:, g * GT:(g + 1) * GT],
                          start=True, stop=True).then_inc(S["logit"], 1)
            for b in range(NB):
                if b % GB == 0:
                    pe.wait_ge(S["st"], b // GB + 1)
                mm = pe.transpose(bank[4][:, b * E:(b + 1) * E], st[0:E, b * P:(b + 1) * P],
                                  k.ident[0:E, 0:E])
            mm.then_inc(S["turn"], 1)
            pe.wait_ge(S["parts"], 1)
            for b in range(NB):
                mm = pe.transpose(bank[b // GB][0:3 * E, (b % GB) * P:(b % GB + 1) * P],
                                  parts[:, b, :, :].rearrange("p q e -> p (q e)"), k.ident[:, :])
                if b % GB == GB - 1:
                    mm.then_inc(S["turn2"], 1)

        @block.scalar
        def _(act):
            for g in range(NG):
                act.wait_ge(S["logit"], g + 1)
                act.activation(st[0:E, g * GT:(g + 1) * GT], bank[g][0:E, :],
                               ACT.Sigmoid if kind == "sigmoid" else ACT.Copy).then_inc(S["st"], 1)
            if kind == "softmax":
                act.wait_ge(S["chain"], 2)
                act.activation(v, s, ACT.Exp).then_inc(S["exp"], 1)
            act.wait_ge(S["sel"], 5)
            for g in range(NG):
                act.wait_ge(S["turn2"], g + 1)
                act.activation(k.combt[0:3 * E, g * GT:(g + 1) * GT], bank[g][0:3 * E, :], ACT.Copy)\
                   .then_inc(S["comb"], 1)

        @block.gpsimd
        def _(pool):
            pool.memset(k.combt[:, :], 0.0).then_inc(S["sel"], 1)
            make_selectors(pool, k, E, width, S["sel"], 1)

        @block.vector
        def _(dve):
            done = [0]

            def link(ins):
                done[0] += 1
                ins.then_inc(S["chain"], 1)
                dve.wait_ge(S["chain"], done[0])

            def ranks(val, r, c, n, span):
                for e in range(span):
                    ins = dve.memset(r[:, :, e::span] if span < n else r[:, :, e:e + 1],
                                     float(span - 1 - e))
                link(ins)
                vv = val.rearrange("p t (g s) -> p (t g) s", s=span)
                rr = r.rearrange("p t (g s) -> p (t g) s", s=span)
                cc = c.rearrange("p t (g s) -> p (t g) s", s=span)
                for o in range(1, span):
                    link(dve.tensor_tensor(cc[:, :, 0:span - o], vv[:, :, 0:span - o], vv[:, :, o:span],
                                           ALU.is_ge))
                    link(dve.tensor_tensor(rr[:, :, 0:span - o], rr[:, :, 0:span - o],
                                           cc[:, :, 0:span - o], ALU.subtract))
                    link(dve.tensor_tensor(rr[:, :, o:span], rr[:, :, o:span], cc[:, :, 0:span - o],
                                           ALU.add))

            dve.wait_ge(S["turn"], 1)
            p_s = bank[4][:, 0:TE].rearrange("p (t e) -> p t e", t=NB)
            if kind == "softmax":
                link(dve.tensor_reduce(tot, p_s, AX.X, ALU.max))
                link(dve.tensor_tensor(s, p_s, tot.unsqueeze(2).broadcast_to([P, NB, E]), ALU.subtract))
                dve.wait_ge(S["exp"], 1)
                link(dve.tensor_reduce(tot, v, AX.X, ALU.add))
                link(dve.reciprocal(tot, tot))
                link(dve.tensor_tensor(s, v, tot.unsqueeze(2).broadcast_to([P, NB, E]), ALU.mult))
                ranks(s, rank, cmp, E, E)
            else:
                link(dve.tensor_copy(s, p_s))
                base = s
                if rbias is not None:
                    link(dve.tensor_tensor(w, s, rbias.unsqueeze(1).broadcast_to([P, NB, E]), ALU.add))
                    base = w
                if rbias is not None:
                    link(dve.tensor_reduce(gsc, base.rearrange("p t (g s) -> p t g s", s=gs), AX.X,
                                           ALU.max))
                else:
                    q = base.rearrange("p t (g s) -> p t g s", s=gs)
                    hi1, lo1, hi2, lo2 = tmp
                    dve.tensor_tensor(hi1, q[:, :, :, 0], q[:, :, :, 1], ALU.max)
                    dve.tensor_tensor(lo1, q[:, :, :, 0], q[:, :, :, 1], ALU.min)
                    dve.tensor_tensor(hi2, q[:, :, :, 2], q[:, :, :, 3], ALU.max)
                    link(dve.tensor_tensor(lo2, q[:, :, :, 2], q[:, :, :, 3], ALU.min))
                    link(dve.tensor_tensor(gsc, hi1, hi2, ALU.max))
                    link(dve.tensor_tensor(hi1, hi1, hi2, ALU.min))
                    link(dve.tensor_tensor(lo1, lo1, lo2, ALU.max))
                    link(dve.tensor_tensor(hi1, hi1, lo1, ALU.max))
                    link(dve.tensor_tensor(gsc, gsc, hi1, ALU.add))
                ranks(gsc, grank, gcmp, G, G)
                link(dve.tensor_scalar(gcmp, grank, float(top_groups), None, ALU.is_lt))
                link(dve.tensor_tensor(v.rearrange("p t (g s) -> p t g s", s=gs),
                                       base.rearrange("p t (g s) -> p t g s", s=gs),
                                       gcmp.unsqueeze(3).broadcast_to([P, NB, G, gs]), ALU.mult))
                ranks(v, rank, cmp, E, E)
            link(dve.tensor_scalar(sel, rank, float(top), None, ALU.is_lt))
            link(dve.tensor_tensor(w, s, sel, ALU.mult))
            if kind == "sigmoid":
                link(dve.tensor_reduce(tot, w, AX.X, ALU.add))
                link(dve.tensor_scalar(tot, tot, 1e-20, None, ALU.add))
                link(dve.reciprocal(tot, tot))
                link(dve.tensor_scalar(tot, tot, factor, None, ALU.mult))
                link(dve.tensor_tensor(w, w, tot.unsqueeze(2).broadcast_to([P, NB, E]), ALU.mult))
            link(dve.tensor_copy(bf, w))
            link(dve.tensor_copy(parts[:, :, 0, :], bf))
            link(dve.tensor_tensor(low, w, parts[:, :, 0, :], ALU.subtract))
            link(dve.tensor_copy(bf, low))
            link(dve.tensor_copy(parts[:, :, 1, :], bf))
            dve.tensor_tensor(parts[:, :, 2, :], low, parts[:, :, 1, :], ALU.subtract)\
               .then_inc(S["parts"], 1)


def prepare_l1(k):
    nc, bank = k.nc, k.bank
    a = Arena(k)
    peak, allpeak, per_step, step_size, spread = (a.take(2) for _ in range(5))
    ones, turned_max = a.take(P), a.take(2)[0:2, 0:1]
    q = [a.take(512), a.take(512)]
    chain, peaked, reduced, lora = (k.sem("l1w_" + n) for n in ("chain", "peak", "reduced", "lora"))
    wfc, wproj = k.w["wfc"], k.w["wproj"]
    with nc.Block() as block:
        @block.vector
        def _(dve):
            done = [0]

            def link(ins):
                done[0] += 1
                ins.then_inc(chain, 1)
                dve.wait_ge(chain, done[0])

            dve.wait_ge(k.late[1], k.late_count[1])
            link(dve.tensor_scalar(k.w["wq1"][:, :], k.w["wq1"][:, :], 0.125, None, ALU.mult))
            dve.memset(ones, 1.0)
            for n, w in enumerate((wfc, wproj)):
                dve.tensor_reduce(peak[:, n:n + 1], w[:, :], AX.X, ALU.max, apply_absolute_value=True)\
                   .then_inc(peaked, 1)
            dve.wait_ge(reduced, 1)
            link(dve.tensor_reduce(turned_max, bank[2][0:2, 0:P], AX.X, ALU.max))
            dve.tensor_scalar(spread[0:2, :], k.ident[0:2, 0:2], turned_max, None, ALU.mult)\
               .then_inc(peaked, 1)
            dve.wait_ge(reduced, 2)
            link(dve.tensor_copy(allpeak, bank[3][:, 0:2]))
            link(dve.tensor_scalar(step_size, allpeak, 1.0 / 127.0, None, ALU.mult))
            link(dve.reciprocal(per_step, step_size))
            for n, w in enumerate((wfc, wproj)):
                link(dve.tensor_scalar(q[n], w[:, :], per_step[:, n:n + 1], None, ALU.mult))
                link(dve.tensor_scalar(q[n], q[n], ROUND, ROUND, ALU.add, ALU.subtract))
                link(dve.tensor_scalar(q[n], q[n], -128.0, 127.0, ALU.max, ALU.min))
                link(dve.scalar_tensor_tensor(out=q[n], in0=q[n], scalar=step_size[:, n:n + 1],
                                              in1=w[:, :], op0=ALU.mult, op1=ALU.subtract))
                link(dve.tensor_tensor(w[:, :], w[:, :], q[n], ALU.add))
            dve.wait_ge(lora, 1)
            for n, w in enumerate((wfc, wproj)):
                link(dve.scalar_tensor_tensor(out=w[:, :], in0=bank[n][:, :], scalar=2.0, in1=w[:, :],
                                              op0=ALU.mult, op1=ALU.add))

        @block.tensor
        def _(pe):
            pe.wait_ge(k.late[1], k.late_count[1])
            pe.matmul(bank[0][:, :], k.w["afc"][:, :], k.w["bfct"][:, :], start=True, stop=True)
            for t in range(4):
                mm = pe.matmul(bank[1][:, t * P:(t + 1) * P], k.w["aproj"][:, t * P:(t + 1) * P],
                               k.w["bprojt"][:, :], start=True, stop=True)
            mm.then_inc(lora, 1)
            pe.wait_ge(peaked, 2)
            pe.transpose(bank[2][0:2, 0:P], peak, k.ident[:, :]).then_inc(reduced, 1)
            pe.wait_ge(peaked, 3)
            pe.matmul(bank[3][:, 0:2], ones[0:2, :], spread[0:2, :], start=True, stop=True)\
              .then_inc(reduced, 1)


def build(nc, dram, out, stages=8):
    ctx = ExitStack()
    with ctx:
        k = Kernel(nc, ctx, dram, out)
        w = k.w
        load_and_constants(k)

        def cut(name, n, width=P):
            return w[name][:, n * width:(n + 1) * width]

        ctxn, lat = k.combined = (k.big[2], k.xnt)
        v0 = k.work[:, 13 * 1024 - 2 * T:].rearrange("p (s c) -> p s c", s=2)
        k.stage(normalise, "n_ctx", k.ctx_tok, k.ctx_tok, ctxn, k.col("ln_x_g"), k.col("ln_x_b"), stats=True)
        k.stage(normalise, "n_x", k.x, k.xn, stats=True)
        k.stage(normalise, "n_lat", k.xn, k.xn, lat, k.col("ln_l_g"), k.col("ln_l_b"), stats=True)
        qn, kl, kc = k.big[0], k.big[1], k.ctx_tok
        k.stage(l0_queries_keys_values, lat, ctxn, qn, kl, kc, v0)
        k.stage(l0_attention, qn, kl, kc, v0)
        if stages > 1:
            k.stage(normalise, "n1", k.x, k.xn, k.xnt)
            k.stage(route, "r0", 16, 4, 2, 4, "sigmoid", w["gate0"][:, :], factor=2.5, width=64)
            tiles = [(cut("up0", j), None, None, k.sels[:, j * P:(j + 1) * P], cut("down0", j))
                     for j in range(8)]
            tiles += [(cut("sup0", j), None, None, None, cut("sdown0", j)) for j in range(2)]
            k.stage(feed_forward, "f0", 1, tiles, ACT.Silu)
        k.stage(load_into_free, [(w["g3"], dram["g3"]), (w["u3"], dram["u3"])])
        if stages > 2:
            k.stage(prepare_l1)
            k.stage(normalise, "n2", k.x, k.xn, k.xnt)
            k.stage(wide_attention, "a1", k.xnt, k.ctxt, k.ctxt, k.big[0])
            k.stage(wide_attention, "b1", k.big[0], k.big[0], k.xnt)
        if stages > 3:
            k.stage(normalise, "n3", k.x, k.xn, k.xnt)
            tiles = [(cut("wfc", j), k.cols[:, C_BFC + j:C_BFC + j + 1], None, None, cut("wproj", j))
                     for j in range(4)]
            k.stage(feed_forward, "f1", 3, tiles, ACT.Gelu)
        if stages > 4:
            k.stage(normalise, "n4", k.x, k.xn, k.xnt)
            k.stage(small_head_attention, "a2", 4, ("wq2", "wk2", "wv2", "wo2"), k.col("bq2"), k.col("bk2"),
                                 k.rows[:, R_BV2:R_BV2 + P], k.mask2,
                                 (0.0, MASKED, ALU.is_equal, ALU.mult), 2)
        k.stage(load_into_free, [(k.mask3, dram["mask3"].broadcast_to([P, T]))])
        if stages > 5:
            k.stage(normalise, "n5", k.x, k.xn, k.xnt)
            k.stage(route, "r2", 8, None, None, 2, "softmax", w["gate2"][:, :], width=128, weights_of=2)
            tiles = [(cut("ew2", j), k.cols[:, C_EB + j:C_EB + j + 1], None,
                      k.sels[:, j * P:(j + 1) * P], w["comb2"][:, :]) for j in range(8)]
            k.stage(feed_forward, "f2", 5, tiles, ACT.Silu)
        if stages > 6:
            k.stage(normalise, "n6", k.x, k.xn, k.xnt)
            k.stage(small_head_attention, "a3", 6, ("wq3", "wk3", "wv3", "wo3"), k.col("bq3"), k.col("bk3"),
                                 k.rows[:, R_BV3:R_BV3 + P], k.mask3,
                                 (-1e9, None, ALU.mult, ALU.bypass), 3)
        if stages > 7:
            k.stage(normalise, "n7", k.x, k.xn, k.xnt)
            k.stage(route, "r3", 32, 8, 4, 6, "sigmoid", w["gate3"][:, :],
                  rbias=k.rows[:, R_SB:R_SB + 32], factor=2.5, width=64, weights_of=3)
            tiles = [(cut("g3", j), None, cut("u3", j), k.sels[:, j * P:(j + 1) * P], cut("down3", j))
                     for j in range(16)]
            tiles += [(w["sg3"][:, :], None, w["su3"][:, :], None, w["sd3"][:, :])]
            k.stage(feed_forward, "f3", 7, tiles, ACT.Silu)
        else:
            stored = k.sem("stored")
            with nc.Block() as block:
                @block.sync
                def _(sp):
                    sp.dma_start(out, k.x[:, :]).then_inc(stored, 16)
                    sp.wait_ge(stored, 16)


def layout(i):
    import numpy as np
    a = {n: np.asarray(v) for n, v in i.items()}

    def t(x):
        return np.ascontiguousarray(x.T)

    def tiles(x):
        n = x.shape[0] // P
        return np.ascontiguousarray(x.reshape(n, P, -1).transpose(1, 0, 2).reshape(P, -1))

    def tok(x):
        return tiles(x.reshape(T, P))

    d = {
        "x": tok(a["x"]), "ctx": tok(a["ctx_1024"]), "ctxt": t(a["ctx_1024"].reshape(T, P)),
        "mask0": a["mask_BxS2_bk0"].reshape(1, T),
        "mask2": np.ascontiguousarray(a["mask_Bx1xSxS2_ik1"].reshape(NB, P, P).transpose(1, 0, 2).reshape(P, T)),
        "mask3": np.ascontiguousarray(a["mask_Bx1x1xS2_ik0"].reshape(1, T)),
        "wq0": a["L0_xattn_W_q"], "wkv0": a["L0_xattn_W_kv"], "wo0": a["L0_xattn_W_out"],
        "gate0": t(a["L0_ffn_gate_weight"]),
        "up0": np.ascontiguousarray(a["L0_ffn_expert_up"].transpose(1, 0, 2).reshape(P, 1024)),
        "down0": tiles(a["L0_ffn_expert_down"].reshape(1024, P)),
        "sup0": a["L0_ffn_shared_up"], "sdown0": tiles(a["L0_ffn_shared_down"]),
        "wq1": a["L1_xattn_Wq"], "wk1": a["L1_xattn_Wk"], "wv1": a["L1_xattn_Wv"],
        "wo1": tiles(a["L1_xattn_Wo"]),
        "wfc": t(a["L1_ffn_W_fc"]), "wproj": tiles(t(a["L1_ffn_W_proj"])),
        "afc": a["L1_ffn_A_fc"], "bfct": t(a["L1_ffn_B_fc"]),
        "aproj": a["L1_ffn_A_proj"], "bprojt": t(a["L1_ffn_B_proj"]),
        "wq2": a["L2_xattn_Wq"], "wk2": a["L2_xattn_Wk"], "wv2": a["L2_xattn_Wv"], "wo2": a["L2_xattn_Wo"],
        "gate2": t(a["L2_ffn_gate_w"]),
        "ew2": np.ascontiguousarray(a["L2_ffn_expert_w"].transpose(2, 0, 1).reshape(P, 1024)),
        "comb2": t(a["L2_ffn_combine_w"]),
        "wq3": a["L3_xattn_wq"], "wk3": a["L3_xattn_wk"], "wv3": a["L3_xattn_wv"], "wo3": a["L3_xattn_wo"],
        "gate3": t(a["L3_ffn_gate_weight"]),
        "g3": np.ascontiguousarray(a["L3_ffn_experts_gate_up"][:, :64].transpose(2, 0, 1).reshape(P, 2048)),
        "u3": np.ascontiguousarray(a["L3_ffn_experts_gate_up"][:, 64:].transpose(2, 0, 1).reshape(P, 2048)),
        "down3": tiles(np.ascontiguousarray(a["L3_ffn_experts_down"].transpose(0, 2, 1)).reshape(2048, P)),
        "sg3": t(a["L3_ffn_shared_gate_w"]), "su3": t(a["L3_ffn_shared_up_w"]),
        "sd3": t(a["L3_ffn_shared_down_w"]),
    }
    cols = [a["L0_xattn_ln_x_g"], a["L0_xattn_ln_x_b"], a["L0_xattn_ln_l_g"], a["L0_xattn_ln_l_b"],
            np.concatenate([a["L0_xattn_q_gamma"]] * 2), np.concatenate([a["L0_xattn_k_gamma"]] * 2),
            a["L0_xattn_b_out"], a["L1_xattn_bo"], a["L1_ffn_b_proj"],
            a["L2_xattn_bq"], a["L2_xattn_bk"], a["L2_xattn_bo"],
            a["L3_xattn_bq"], a["L3_xattn_bk"], a["L3_xattn_bo"]]
    cols += list(a["L1_ffn_b_fc"].reshape(4, P)) + list(a["L2_ffn_expert_b"])
    d["cols"] = np.ascontiguousarray(np.stack(cols, axis=1))
    gates = np.stack([a["g_xattn"], a["g_ffn"]], axis=1).reshape(8)
    row = np.concatenate([gates, a["L2_xattn_bv"], a["L3_xattn_bv"], a["L3_ffn_e_score_correction_bias"]])
    d["rows"] = np.ascontiguousarray(np.broadcast_to(row, (P, NROW)))
    return {n: np.ascontiguousarray(v) for n, v in d.items()}


def kernel(**inputs):
    import numpy as np
    import concourse.bacc as bacc
    from concourse.bass_utils import run_bass_kernel_spmd

    nc = bacc.Bacc("TRN2", target_bir_lowering=False, num_devices=1)
    arrays = {f"in_{n}": v for n, v in layout(inputs).items()}
    dram = {n[3:]: nc.dram_tensor(n, v.shape, mybir.dt.from_np(v.dtype), kind="ExternalInput").ap()
            for n, v in arrays.items()}
    out = nc.dram_tensor("out", (P, T), F32, kind="ExternalOutput").ap()
    build(nc, dram, out)
    r = run_bass_kernel_spmd(nc, [arrays], core_ids=[0])
    got = np.asarray(r.results[0]["out"])
    return np.ascontiguousarray(got.reshape(P, NB, P).transpose(1, 0, 2))
```

```python
import concourse.bass as bass
from concourse import mybir
from contextlib import ExitStack

F32 = mybir.dt.float32
BF16 = mybir.dt.bfloat16
I32 = mybir.dt.int32
U8 = mybir.dt.uint8
ALU = mybir.AluOpType
ACT = mybir.ActivationFunctionType
AX = mybir.AxisListType

P = 128
NB = 16
T = NB * P
GB = 4
NG = NB // GB
GT = GB * P
LN_EPS = 1e-5
MASKED = -float(2.0 ** 100)
ROUND = 12582912.0

COLS = ["ln_x_g", "ln_x_b", "ln_l_g", "ln_l_b", "q_gamma", "k_gamma", "b_out0", "bo1", "b_proj",
        "bq2", "bk2", "bo2", "bq3", "bk3", "bo3"]
COL = {n: i for i, n in enumerate(COLS)}
C_BFC = len(COLS)
C_EB = C_BFC + 4
NCOL = C_EB + 8
R_G, R_BV2, R_BV3, R_SB = 0, 8, 8 + P, 8 + 2 * P
NROW = R_SB + 32


def peeled(eng, n_outer, per, step, longest_lag):
    first = 1 + -(-longest_lag // per)
    for i in range(first):
        for j in range(per):
            step(i, j)
    with eng.Fori(first, n_outer) as i:
        for j in range(per):
            step(i, j)
    for j in range(longest_lag):
        step(n_outer, j)


def back(i, j, lag, per, n_outer):
    j -= lag
    while j < 0:
        i, j = i - 1, j + per
    if isinstance(i, int) and not 0 <= i < n_outer:
        return None
    return i, j


def wait_count(eng, sem, n):
    if isinstance(n, int) and n <= 0:
        return
    eng.wait_ge(sem, n)


class Kernel:

    def __init__(self, nc, ctx, dram, out):
        self.nc, self.ctx, self.dram, self.out = nc, ctx, dram, out
        self.psum = ctx.enter_context(nc.psum_tensor("psum", [P, 8, 512], F32))
        self.bank = [self.psum[:, i, :] for i in range(8)]
        sb = self.sb
        self.x = sb("x", [P, T])
        self.xnt = sb("xnt", [P, T])
        self.ctx_tok = sb("ctx_tok", [P, T])
        self.ctxt = sb("ctxt", [P, T])
        self.big = [sb(f"big{i}", [P, T]) for i in range(3)]
        self.negb = sb("negb", [P, T])
        self.ident = sb("ident", [P, P])
        self.headmask8 = sb("headmask8", [P, 16])
        self.headmask64 = sb("headmask64", [P, 2])
        self.cols = sb("cols", [P, NCOL])
        self.rows = sb("rows", [P, NROW])
        self.gate = sb("gate", [P, 8])
        self.gbias = sb("gbias", [P, 8])
        self.mv = sb("mv", [P, NB * 2])
        self.bn = sb("bn", [P, 2 * 6])
        self.x_new = sb("x_new", [P, 2, P])
        self.mv_new = sb("mv_new", [P, 2, 2])
        self.rstd = sb("rstd", [P, 5 * NB])
        self.mask0 = sb("mask0", [P, T], U8)
        self.mask2 = sb("mask2", [P, T], I32)
        self.mask3 = self.mask2
        self.w = {}
        self.sels = sb("sels", [P, 2048], BF16)
        self.combt = sb("combt", [P, T], BF16)
        self.own, self.cleared = [], []
        self.work = sb("work", [P, 13 * 1024])
        self.xn = self.work[:, 0:T]
        self.tail_bias = {0: "b_out0", 2: "bo1", 3: "b_proj", 4: "bo2", 6: "bo3"}

    def sb(self, name, shape, dt=F32):
        return self.ctx.enter_context(self.nc.sbuf_tensor(name, shape, dt))

    def sem(self, name):
        one = self.nc.alloc_semaphore(name)
        self.own.append(one)
        return one

    def stage(self, make, *args, **named):
        self.own = []
        make(self, *args, **named)
        for one in self.own:
            self.nc.gpsimd.sem_clear(one)
        for one in self.cleared:
            self.nc.release_semaphore(one)
        self.cleared = self.own

    def col(self, name):
        return self.cols[:, COL[name]:COL[name] + 1]


class Arena:

    def __init__(self, k):
        self.k, self.at = k, 0

    def take(self, words, pattern=None, **sizes):
        a = self.k.work[:, self.at:self.at + words]
        self.at += words
        assert self.at <= 13 * 1024, self.at
        return a.rearrange(pattern, **sizes) if pattern else a


WEIGHTS = {
    "wq0": 128, "wkv0": 256, "wo0": 128,
    "gate0": 16, "up0": 1024, "down0": 1024, "sup0": 256, "sdown0": 256,
    "wq1": 1024, "wk1": 1024, "wv1": 1024, "wo1": 1024,
    "wfc": 512, "wproj": 512,
    "wq2": 128, "wk2": 128, "wv2": 128, "wo2": 128,
    "gate2": 8, "ew2": 1024, "comb2": 128,
    "wq3": 128, "wk3": 128, "wv3": 128, "wo3": 128,
    "gate3": 32, "g3": 2048, "u3": 2048, "down3": 2048, "sg3": 128, "su3": 128, "sd3": 128,
}
SMALL = {"afc": (16, 128), "bfct": (16, 512), "aproj": (16, 512), "bprojt": (16, 128)}


def load_weights(k, sp, layers):
    for s in layers:
        for n in [*WEIGHTS, *SMALL]:
            if (int(n[-1]) if n[-1] in "0123" else 1) == s and n not in ("g3", "u3"):
                sp.dma_start(k.w[n][:, :], k.dram[n]).then_inc(k.late[s], 16)
                k.late_count[s] += 16
        if s == 2:
            sp.dma_start(k.mask2[:, :], k.dram["mask2"]).then_inc(k.late[s], 16)
            k.late_count[s] += 16


def load_and_constants(k):
    nc, d = k.nc, k.dram
    k.early = early = k.sem("early_loads")
    k.late = {}
    made, conv, tanh_done = k.sem("consts_made"), k.sem("consts_dve"), k.sem("gates_ready")
    early_loads = [(k.x, "x"), (k.ctx_tok, "ctx"), (k.cols, "cols"), (k.rows, "rows")]
    for n, width in WEIGHTS.items():
        k.w[n] = {"g3": k.ctx_tok, "u3": k.big[1]}.get(n) or k.sb("w_" + n, [P, width])
    for n, shape in SMALL.items():
        k.w[n] = k.sb("w_" + n, list(shape))
    for s in range(4):
        k.late[s] = k.sem(f"weights{s}_loaded")
    k.late_count = {s: 0 for s in range(4)}
    ctxt_loaded = k.ctxt_loaded = k.sem("ctxt_loaded")

    with nc.Block() as block:
        @block.sync
        def _(sp):
            for dst, name in early_loads:
                src = d[name]
                sp.dma_start(dst[:, :], src).then_inc(early, 16)
            sp.dma_start(k.mask0[:, :], d["mask0"].broadcast_to([P, T])).then_inc(k.late[0], 16)
            sp.dma_start(k.ctxt[:, :], d["ctxt"]).then_inc(ctxt_loaded, 16)
            k.late_count[0] += 16
            load_weights(k, sp, [0])

        @block.gpsimd
        def _(pool):
            pool.memset(k.ident[:, :], 0.0).then_inc(made, 1)
            pool.memset(k.headmask8[:, :], 1.0).then_inc(made, 1)
            pool.memset(k.headmask64[:, :], 1.0).then_inc(made, 1)
            pool.wait_ge(made, 3)
            pool.affine_select(out=k.ident[:, :], in_=k.ident[:, :], compare_op=ALU.not_equal, fill=1.0,
                               base=0, pattern=[[-1, P]], channel_multiplier=1).then_inc(made, 1)
            for n, (m, width, heads, last) in enumerate([(k.headmask8, 8, 16, None),
                                                         (k.headmask64, 64, 2, None)]):
                pool.affine_select(out=m[:, :], in_=m[:, :], compare_op=ALU.is_ge, fill=0.0,
                                   base=0, pattern=[[-width, heads]], channel_multiplier=1).then_inc(made, 1)
                pool.wait_ge(made, 5 + 2 * n)
                pool.affine_select(out=m[:, :], in_=m[:, :], compare_op=ALU.is_ge, fill=0.0,
                                   base=width - 1, pattern=[[width, heads]],
                                   channel_multiplier=-1).then_inc(made, 1)

        @block.scalar
        def _(act):
            act.wait_ge(early, 64)
            act.activation(k.gate[:, :], k.rows[:, R_G:R_G + 8], ACT.Tanh).then_inc(tanh_done, 1)

        @block.vector
        def _(dve):
            dve.memset(k.gbias[:, :], 0.0).then_inc(conv, 1)
            dve.wait_ge(tanh_done, 1)
            dve.wait_ge(conv, 1)
            for s, name in k.tail_bias.items():
                dve.tensor_tensor(k.gbias[:, s:s + 1], k.gate[:, s:s + 1], k.col(name), ALU.mult)\
                   .then_inc(conv, 1)
            dve.wait_ge(early, 64)
            dve.tensor_scalar(k.col("q_gamma"), k.col("q_gamma"), 0.125, None, ALU.mult).then_inc(conv, 1)
            for name in ("bq2", "bq3"):
                dve.tensor_scalar(k.col(name), k.col(name), 8.0 ** -0.5, None, ALU.mult).then_inc(conv, 1)


def load_into_free(k, block, pairs):
    @block.sync
    def _(sp):
        sp.wait_ge(k.late[2], k.late_count[2])
        for dst, src in pairs:
            sp.dma_start(dst[:, :], src).then_inc(k.late[3], 16)
            k.late_count[3] += 16


def normalise(k, tag, src, dst, dst_t=None, gain=None, bias=None, stats=False, twice=False, loads=()):
    nc = k.nc
    chain, rooted = k.sem(f"{tag}_chain"), k.sem(f"{tag}_std")
    normed, turned, copied = k.sem(f"{tag}_normed"), k.sem(f"{tag}_turned"), k.sem(f"{tag}_copied")
    mv = k.mv[:, :].rearrange("p (b two) -> p b two", two=2)
    var, std, r, t, r2 = (k.rstd[:, n * NB:(n + 1) * NB] for n in range(5))
    with nc.Block() as block:
        if loads:
            load_into_free(k, block, loads)

        @block.vector
        def _(dve):
            done = [0]

            def link(ins):
                done[0] += 1
                ins.then_inc(chain, 1)
                dve.wait_ge(chain, done[0])

            if stats:
                bn = k.work[:, 12 * 1024:12 * 1024 + 6 * NB].rearrange("p (b c) -> p b c", b=NB)
                for b in range(NB):
                    ins = dve.bn_stats(bn[:, b, :], src[:, b * P:(b + 1) * P])
                link(ins)
                for b in range(NB):
                    ins = dve.bn_aggr(mv[:, b, :], bn[:, b, :])
                link(ins)
            link(dve.tensor_scalar(var, mv[:, :, 1], LN_EPS, None, ALU.add))
            dve.wait_ge(rooted, 1)
            link(dve.reciprocal(r, std))
            link(dve.tensor_tensor(t, r, r, ALU.mult))
            link(dve.tensor_tensor(t, t, var, ALU.mult))
            link(dve.tensor_scalar(t, t, -0.5, 1.5, ALU.mult, ALU.add))
            link(dve.tensor_tensor(r, r, t, ALU.mult))
            if twice:
                link(dve.tensor_tensor(t, r, r, ALU.mult))
                link(dve.tensor_tensor(t, t, mv[:, :, 1], ALU.mult))
                link(dve.tensor_scalar(var, t, LN_EPS, None, ALU.add))
                dve.wait_ge(rooted, 2)
                link(dve.reciprocal(r2, std))
                link(dve.tensor_tensor(t, r2, r2, ALU.mult))
                link(dve.tensor_tensor(t, t, var, ALU.mult))
                link(dve.tensor_scalar(t, t, -0.5, 1.5, ALU.mult, ALU.add))
                link(dve.tensor_tensor(r2, r2, t, ALU.mult))
                link(dve.tensor_tensor(r, r, r2, ALU.mult))
            for b in range(NB):
                s = slice(b * P, (b + 1) * P)
                dve.tensor_scalar(dst[:, s], src[:, s], mv[:, b, 0:1], r[:, b:b + 1],
                                  ALU.subtract, ALU.mult).then_inc(normed, 1)

        @block.scalar
        def _(act):
            act.wait_ge(chain, (2 if stats else 0) + 1)
            act.activation(std, var, ACT.Sqrt).then_inc(rooted, 1)
            if twice:
                act.wait_ge(chain, (2 if stats else 0) + 9)
                act.activation(std, var, ACT.Sqrt).then_inc(rooted, 1)
            if dst_t is not None:
                for g in range(NG):
                    act.wait_ge(turned, g + 1)
                    act.activation(dst_t[:, g * GT:(g + 1) * GT], k.bank[g][:, :], ACT.Identity,
                                   scale=gain if gain is not None else 1.0,
                                   bias=bias if bias is not None else 0.0).then_inc(copied, 1)

        @block.tensor
        def _(pe):
            if dst_t is not None:
                for b in range(NB):
                    pe.wait_ge(normed, b + 1)
                    mm = pe.transpose(k.bank[b // GB][:, (b % GB) * P:(b % GB + 1) * P],
                                      dst[:, b * P:(b + 1) * P], k.ident[:, :])
                    if b % GB == GB - 1:
                        mm.then_inc(turned, 1)


def residual(k, dve, sub, b, psum, added, stated, slot, n):
    xb = k.x[:, bass.ds(b * P, P)]
    if sub == 7:
        dve.tensor_tensor(xb, psum, xb, ALU.add).then_inc(added, 1)
        return
    new, bn, mean_var = k.x_new[:, slot, :], k.bn[:, 6 * slot:6 * slot + 6], k.mv_new[:, slot, :]
    dve.tensor_tensor(new, psum, xb, ALU.add).then_inc(added, 1)
    dve.wait_ge(added, n + 1)
    dve.bn_stats(bn, new).then_inc(stated, 1)
    dve.wait_ge(stated, 2 * n + 1)
    dve.tensor_scalar(xb, new, 1.0, None, ALU.mult)
    dve.bn_aggr(mean_var, bn).then_inc(stated, 1)
    dve.wait_ge(stated, 2 * n + 2)
    dve.tensor_scalar(k.mv[:, bass.ds(b * 2, 2)], mean_var, 1.0, None, ALU.mult)



def l0_queries_keys_values(k, lat_t, ctxn_t, qn, kl, kc, v):
    nc, bank = k.nc, k.bank
    a = Arena(k)
    sq = a.take(2 * 3 * P, "p (n c) -> p n c", n=2)
    total, root, inv = (a.take(12, "p (n h) -> p n h", n=2) for _ in range(3))
    normed = a.take(2 * 3 * P, "p (n c) -> p n c", n=2)
    S = {n: k.sem("l0p_" + n) for n in
         ("proj", "sq", "total", "root", "guard", "inv", "scaled", "turn", "copied")}
    wq, wkv = k.w["wq0"], k.w["wkv0"]

    def heads(x):
        return x.rearrange("p (h c) -> p h c", c=64)

    with nc.Block() as block:
        @block.sync
        def _(sp):
            load_weights(k, sp, [1, 2, 3])

        @block.tensor
        def _(pe):
            pe.wait_ge(k.late[0], k.late_count[0])
            for n in range(NB + 2):
                if n < NB:
                    own, other, s = bank[n % 2], bank[2 + n % 2], slice(n * P, (n + 1) * P)
                    if n >= 2:
                        pe.wait_ge(S["scaled"], n - 1)
                    pe.matmul(own[:, 0:P], lat_t[:, s], wq[:, :], start=True, stop=True)
                    pe.matmul(own[:, P:3 * P], lat_t[:, s], wkv[:, :], start=True, stop=True)
                    pe.matmul(other[:, 0:2 * P], ctxn_t[:, s], wkv[:, :], start=True, stop=True)\
                      .then_inc(S["proj"], 1)
                if n >= 2:
                    m = n - 2
                    pe.wait_ge(S["scaled"], m + 1)
                    if m >= 2:
                        pe.wait_ge(S["copied"], m - 1)
                    for part in range(3):
                        c = slice(part * P, (part + 1) * P)
                        mm = pe.transpose(bank[4 + m % 2][:, c], normed[:, m % 2, c], k.ident[:, :])
                    mm.then_inc(S["turn"], 1)

        @block.scalar
        def _(act):
            for n in range(NB + 2):
                if 1 <= n <= NB:
                    m = n - 1
                    act.wait_ge(S["total"], m + 1)
                    if m >= 2:
                        act.wait_ge(S["guard"], m - 1)
                    act.activation(root[:, m % 2, :], total[:, m % 2, :], ACT.Sqrt, scale=1.0 / 64)\
                       .then_inc(S["root"], 1)
                if n < NB:
                    act.wait_ge(S["proj"], n + 1)
                    if n >= 2:
                        act.wait_ge(S["total"], n - 1)
                    act.activation(sq[:, n % 2, 0:2 * P], bank[n % 2][:, 0:2 * P], ACT.Square)
                    act.activation(sq[:, n % 2, 2 * P:3 * P], bank[2 + n % 2][:, 0:P], ACT.Square)\
                       .then_inc(S["sq"], 1)
                if n >= 2:
                    m = n - 2
                    act.wait_ge(S["turn"], m + 1)
                    for part, (dst, gamma) in enumerate(((qn, "q_gamma"), (kl, "k_gamma"),
                                                         (kc, "k_gamma"))):
                        ins = act.activation(dst[:, m * P:(m + 1) * P],
                                             bank[4 + m % 2][:, part * P:(part + 1) * P], ACT.Copy,
                                             scale=k.col(gamma))
                    ins.then_inc(S["copied"], 1)

        @block.vector
        def _(dve):
            dve.wait_ge(k.late[0], k.late_count[0])
            dve.tensor_scalar(k.negb[:, :], k.mask0[:, :], 0.0, MASKED, ALU.is_equal, ALU.mult)
            for n in range(NB + 1):
                if n >= 1:
                    m = n - 1
                    own, other, i = bank[m % 2], bank[2 + m % 2], inv[:, m % 2, :]
                    dve.tensor_copy(v[:, 1, m * P:(m + 1) * P], own[:, 2 * P:3 * P])
                    dve.tensor_copy(v[:, 0, m * P:(m + 1) * P], other[:, P:2 * P])
                    dve.wait_ge(S["root"], m + 1)
                    dve.tensor_scalar(i, root[:, m % 2, :], 1e-8, None, ALU.max).then_inc(S["guard"], 1)
                    dve.wait_ge(S["guard"], m + 1)
                    dve.reciprocal(i, i).then_inc(S["inv"], 1)
                    dve.wait_ge(S["inv"], m + 1)
                    if m >= 2:
                        dve.wait_ge(S["turn"], m - 1)
                    dve.tensor_tensor(heads(normed[:, m % 2, 0:2 * P]), heads(own[:, 0:2 * P]),
                                      i[:, 0:4].unsqueeze(2).broadcast_to([P, 4, 64]), ALU.mult)
                    dve.tensor_tensor(heads(normed[:, m % 2, 2 * P:3 * P]), heads(other[:, 0:P]),
                                      i[:, 4:6].unsqueeze(2).broadcast_to([P, 2, 64]), ALU.mult)\
                       .then_inc(S["scaled"], 1)
                if n < NB:
                    dve.wait_ge(S["sq"], n + 1)
                    if n >= 2:
                        dve.wait_ge(S["root"], n - 1)
                    dve.tensor_reduce(total[:, n % 2, :], heads(sq[:, n % 2, :]), AX.X, ALU.add)\
                       .then_inc(S["total"], 1)


def l0_attention(k, qn, kl, kc, v):
    nc, bank, sub = k.nc, k.bank, 0
    a = Arena(k)
    qm = a.take(2 * 256, "p (n h c) -> p n h c", n=2, h=2)
    prob = a.take(2 * 512, "p (n c) -> p n c", n=2)
    probt = a.take(2 * 512, "p (n c) -> p n c", n=2)
    nmax = a.take(4, "p (n h) -> p n h", n=2)
    rsum = a.take(4, "p (n h) -> p n h", n=2)
    rinv = a.take(4, "p (n h) -> p n h", n=2)
    on = a.take(P)
    ot = a.take(P)
    yt = a.take(P)
    S = {n: k.sem("l0a_" + n) for n in
         ("qm", "score", "mask", "max", "exp", "turn", "pt", "pv", "inv", "on", "tail1", "ot",
          "proj", "yt", "tail2", "added", "stated")}
    per = 2

    def num(i, j):
        return i * per + j

    tail = Tail(k, S, sub, num, on, ot, yt, k.w["wo0"], 6)

    with nc.Block() as block:
        @block.tensor
        def _(pe):
            def step(i, j):
                if at := back(i, j, 1, per, NB // per):
                    n, c = num(*at), at[1]
                    pe.wait_ge(S["qm"], (n + 1) * 2)
                    wait_count(pe, S["exp"], (n - 1) * 2)
                    for h in range(2):
                        for half, keys in enumerate((kc, kl)):
                            mm = pe.matmul(bank[c][:, h * 256 + half * P:h * 256 + (half + 1) * P],
                                           qm[:, c, h, :], keys[:, bass.ds(n * P, P)],
                                           start=True, stop=True)
                    mm.then_inc(S["score"], 1)
                if at := back(i, j, 3, per, NB // per):
                    n, c = num(*at), at[1]
                    pe.wait_ge(S["exp"], (n + 1) * 2)
                    wait_count(pe, S["pt"], n - 1)
                    for q in range(4):
                        mm = pe.transpose(bank[2 + c][:, q * P:(q + 1) * P],
                                          prob[:, c, q * P:(q + 1) * P], k.ident[:, :])
                    mm.then_inc(S["turn"], 1)
                if at := back(i, j, 4, per, NB // per):
                    n, c = num(*at), at[1]
                    pe.wait_ge(S["pt"], n + 1)
                    wait_count(pe, S["on"], n)
                    for h in range(2):
                        for half in range(2):
                            q = 2 * h + half
                            mm = pe.matmul(bank[4][:, h * 64:(h + 1) * 64],
                                           probt[:, c, q * P:(q + 1) * P],
                                           v[:, half, bass.ds(n * P + h * 64, 64)],
                                           start=(half == 0), stop=(half == 1))
                    mm.then_inc(S["pv"], 1)
                tail.pe_turn(pe, back(i, j, 5, per, NB // per))
                tail.pe_project(pe, back(i, j, 6, per, NB // per))
                tail.pe_back(pe, back(i, j, 7, per, NB // per))
            peeled(pe, NB // per, per, step, 8)

        @block.scalar
        def _(act):
            def step(i, j):
                if at := back(i, j, 2, per, NB // per):
                    n, c = num(*at), at[1]
                    act.wait_ge(S["max"], n + 1)
                    wait_count(act, S["turn"], n - 1)
                    wait_count(act, S["inv"], n - 1)
                    for h in range(2):
                        act.activation(prob[:, c, h * 256:(h + 1) * 256], bank[c][:, h * 256:(h + 1) * 256],
                                       ACT.Exp, bias=nmax[:, c, h:h + 1],
                                       accum_out=rsum[:, c, h:h + 1]).then_inc(S["exp"], 1)
                if at := back(i, j, 3, per, NB // per):
                    n, c = num(*at), at[1]
                    act.wait_ge(S["turn"], n + 1)
                    wait_count(act, S["pv"], n - 1)
                    act.activation(probt[:, c, :], bank[2 + c][:, :], ACT.Copy).then_inc(S["pt"], 1)
                if at := back(i, j, 0, per, NB // per):
                    n, c = num(*at), at[1]
                    wait_count(act, S["score"], n - 1)
                    for h in range(2):
                        act.activation(qm[:, c, h, :], qn[:, bass.ds(n * P, P)], ACT.Copy,
                                       scale=k.headmask64[:, h:h + 1]).then_inc(S["qm"], 1)
                tail.act_turn(act, back(i, j, 5, per, NB // per))
                tail.act_project(act, back(i, j, 6, per, NB // per))
            peeled(act, NB // per, per, step, 7)

        @block.vector
        def _(dve):
            def step(i, j):
                if at := back(i, j, 1, per, NB // per):
                    n, c = num(*at), at[1]
                    dve.wait_ge(S["score"], n + 1)
                    s = bank[c][:, :].rearrange("p (h w) -> p h w", h=2)
                    dve.tensor_tensor(s[:, :, 0:P], s[:, :, 0:P],
                                      k.negb[:, bass.ds(n * P, P)].unsqueeze(1).broadcast_to([P, 2, P]),
                                      ALU.add).then_inc(S["mask"], 1)
                    dve.wait_ge(S["mask"], n + 1)
                    wait_count(dve, S["exp"], (n - 1) * 2)
                    dve.tensor_reduce(nmax[:, c, :], s, AX.X, ALU.max, negate=True).then_inc(S["max"], 1)
                if at := back(i, j, 3, per, NB // per):
                    n, c = num(*at), at[1]
                    dve.wait_ge(S["exp"], (n + 1) * 2)
                    dve.reciprocal(rinv[:, c, :], rsum[:, c, :]).then_inc(S["inv"], 1)
                if at := back(i, j, 4, per, NB // per):
                    n, c = num(*at), at[1]
                    dve.wait_ge(S["inv"], n + 1)
                    dve.wait_ge(S["pv"], n + 1)
                    wait_count(dve, S["tail1"], n)
                    dve.tensor_tensor(on.rearrange("p (h c) -> p h c", h=2),
                                      bank[4][:, 0:P].rearrange("p (h c) -> p h c", h=2),
                                      rinv[:, c, :].unsqueeze(2).broadcast_to([P, 2, 64]), ALU.mult)\
                       .then_inc(S["on"], 1)
                tail.dve_add(dve, back(i, j, 7, per, NB // per))
            peeled(dve, NB // per, per, step, 8)


class Tail:

    def __init__(self, k, S, sub, num, on, ot, yt, wo, proj_bank):
        self.k, self.S, self.sub, self.num = k, S, sub, num
        self.on, self.ot, self.yt, self.wo = on, ot, yt, wo
        self.turned, self.proj, self.back = k.bank[5], k.bank[proj_bank], k.bank[7]

    def pe_turn(self, pe, at):
        if at:
            n, S = self.num(*at), self.S
            pe.wait_ge(S["on"], n + 1)
            wait_count(pe, S["ot"], n)
            if self.proj is self.turned:
                wait_count(pe, S["yt"], n)
            pe.transpose(self.turned[:, 0:P], self.on, self.k.ident[:, :]).then_inc(S["tail1"], 1)

    def act_turn(self, act, at):
        if at:
            n, S = self.num(*at), self.S
            act.wait_ge(S["tail1"], n + 1)
            wait_count(act, S["proj"], n)
            act.activation(self.ot, self.turned[:, 0:P], ACT.Copy).then_inc(S["ot"], 1)

    def pe_project(self, pe, at):
        if at:
            n, S = self.num(*at), self.S
            pe.wait_ge(S["ot"], n + 1)
            wait_count(pe, S["yt"], n)
            pe.matmul(self.proj[:, 0:P], self.wo[:, :], self.ot, start=True, stop=True)\
              .then_inc(S["proj"], 1)

    def act_project(self, act, at):
        if at:
            n, S, sub, k = self.num(*at), self.S, self.sub, self.k
            act.wait_ge(S["proj"], n + 1)
            wait_count(act, S["tail2"], n)
            act.activation(self.yt, self.proj[:, 0:P], ACT.Identity, scale=k.gate[:, sub:sub + 1],
                           bias=k.gbias[:, sub:sub + 1]).then_inc(S["yt"], 1)

    def pe_back(self, pe, at):
        if at:
            n, S = self.num(*at), self.S
            pe.wait_ge(S["yt"], n + 1)
            wait_count(pe, S["added"], n)
            pe.transpose(self.back[:, 0:P], self.yt, self.k.ident[:, :]).then_inc(S["tail2"], 1)

    def dve_add(self, dve, at):
        if at:
            n, S = self.num(*at), self.S
            dve.wait_ge(S["tail2"], n + 1)
            residual(self.k, dve, self.sub, n, self.back[:, 0:P], S["added"], S["stated"], 0, n)



def small_head_attention(k, tag, sub, names, bias_q, bias_k, bv, mask, mask_ops, weights_of):
    nc, bank = k.nc, k.bank
    a = Arena(k)
    qt = a.take(2 * P, "p (n c) -> p n c", n=2)
    kt = a.take(2 * P, "p (n c) -> p n c", n=2)
    cs = a.take(2 * P, "p (n c) -> p n c", n=2)
    km = a.take(2 * T, "p (n h c) -> p n h c", n=2, h=16)
    v = a.take(2 * 144, "p (n h c) -> p n h c", n=2, h=16)
    score = a.take(2 * 512, "p (n h c) -> p n h c", n=2, h=4)
    prob = a.take(2 * 512, "p (n c) -> p n c", n=2)
    probt = a.take(2 * 512, "p (n c) -> p n c", n=2)
    nmax = a.take(8, "p (n h) -> p n h", n=2)
    rinv = a.take(16)
    on = a.take(P)
    ot = a.take(P)
    yt = a.take(P)
    S = {n: k.sem(f"{tag}_" + n) for n in
         ("cs", "projqk", "projv", "proj", "qt", "kt", "v", "km", "score", "mask", "max", "exp", "turn", "pt", "pv",
          "inv", "on", "tail1", "ot", "yt", "tail2", "added", "stated", "setup")}
    wq, wk, wv, wo = (k.w[n] for n in names)
    CH = 4
    per, outer = 2 * CH, NB // 2
    scale = 8.0 ** -0.5

    def seq(i, j):
        return i * 2 + j // CH

    def ends(at):
        return at if at and at[1] % CH == CH - 1 else None

    tail = Tail(k, S, sub, seq, on, ot, yt, wo, 5)

    with nc.Block() as block:
        @block.tensor
        def _(pe):
            pe.wait_ge(k.late[weights_of], k.late_count[weights_of])

            def step(i, j):
                if (at := back(i, j, 0, per, outer)) and at[1] % CH == 0:
                    b, c = seq(*at), at[1] // CH
                    wait_count(pe, S["v"], b)
                    pe.wait_ge(S["cs"], b + 1)
                    pe.matmul(bank[0][:, 0:P], wq[:, :], k.xnt[:, bass.ds(b * P, P)],
                              start=True, stop=True)
                    pe.matmul(bank[0][:, P:2 * P], wk[:, :], cs[:, c, :], start=True, stop=True)\
                      .then_inc(S["projqk"], 1)
                if (at := back(i, j, 2, per, outer)) and at[1] % CH == 0:
                    b, c = seq(*at), at[1] // CH
                    pe.wait_ge(S["qt"], b + 1)
                    pe.matmul(bank[0][:, 2 * P:3 * P], cs[:, c, :], wv[:, :], start=True, stop=True)\
                      .then_inc(S["projv"], 1)
                if at := back(i, j, 4, per, outer):
                    n, b, c = at[0] * per + at[1], seq(*at), at[1] % CH
                    if c == 0:
                        pe.wait_ge(S["km"], b + 1)
                        pe.wait_ge(S["qt"], b + 1)
                    wait_count(pe, S["mask"], n - 1)
                    pe.matmul(bank[1 + at[1] % 2][:, :], qt[:, at[1] // CH, :],
                              km[:, at[1] // CH, 4 * c:4 * c + 4, :].rearrange("p h c -> p (h c)"),
                              start=True, stop=True).then_inc(S["score"], 1)
                if at := back(i, j, 6, per, outer):
                    n = at[0] * per + at[1]
                    pe.wait_ge(S["exp"], (n + 1) * 4)
                    wait_count(pe, S["pt"], n - 1)
                    for h in range(4):
                        mm = pe.transpose(bank[(3, 6)[at[1] % 2]][:, h * P:(h + 1) * P],
                                          prob[:, at[1] % 2, h * P:(h + 1) * P], k.ident[:, :])
                    mm.then_inc(S["turn"], 1)
                if at := back(i, j, 7, per, outer):
                    n, b, c = at[0] * per + at[1], seq(*at), at[1] % CH
                    pe.wait_ge(S["pt"], n + 1)
                    if c == 0:
                        pe.wait_ge(S["v"], b + 1)
                        wait_count(pe, S["on"], b)
                    for h in range(4):
                        hh = 4 * c + h
                        mm = pe.matmul(bank[4][:, hh * 9:(hh + 1) * 9],
                                       probt[:, at[1] % 2, h * P:(h + 1) * P],
                                       v[:, at[1] // CH, hh, :], start=True, stop=True)
                    mm.then_inc(S["pv"], 1)
                tail.pe_turn(pe, ends(back(i, j, 8, per, outer)))
                tail.pe_project(pe, ends(back(i, j, 9, per, outer)))
                tail.pe_back(pe, ends(back(i, j, 10, per, outer)))
            peeled(pe, outer, per, step, 11)

        @block.gpsimd
        def _(pool):
            pool.wait_ge(k.ctxt_loaded, 16)

            def step(i, j):
                if (at := back(i, j, 0, per, outer)) and at[1] % CH == 0:
                    b, c = seq(*at), at[1] // CH
                    wait_count(pool, S["projv"], b - 1)
                    pool.tensor_copy(cs[:, c, :], k.ctxt[:, bass.ds(b * P, P)]).then_inc(S["cs"], 1)
                    pool.wait_ge(S["kt"], b + 1)
                    wait_count(pool, S["score"], (b - 1) * CH)
                    pool.tensor_tensor(km[:, c, :, :], kt[:, c, :].unsqueeze(1).broadcast_to([P, 16, P]),
                                       k.headmask8[:, :].unsqueeze(2).broadcast_to([P, 16, P]),
                                       ALU.mult).then_inc(S["km"], 1)
            peeled(pool, outer, per, step, 0)

        @block.scalar
        def _(act):
            def step(i, j):
                if (at := back(i, j, 0, per, outer)) and at[1] % CH == 0:
                    b, c = seq(*at), at[1] // CH
                    act.wait_ge(S["projqk"], b + 1)
                    wait_count(act, S["km"], b - 1)
                    act.activation(kt[:, c, :], bank[0][:, P:2 * P], ACT.Identity, bias=bias_k)\
                       .then_inc(S["kt"], 1)
                    wait_count(act, S["score"], (b - 1) * CH)
                    act.activation(qt[:, c, :], bank[0][:, 0:P], ACT.Identity, scale=scale, bias=bias_q)\
                       .then_inc(S["qt"], 1)
                if at := back(i, j, 5, per, outer):
                    n, m = at[0] * per + at[1], at[1] % 2
                    act.wait_ge(S["max"], n + 1)
                    wait_count(act, S["turn"], n - 1)
                    for h in range(4):
                        act.activation(prob[:, m, h * P:(h + 1) * P], score[:, m, h, :], ACT.Exp,
                                       bias=nmax[:, m, h:h + 1]).then_inc(S["exp"], 1)
                if at := back(i, j, 6, per, outer):
                    n = at[0] * per + at[1]
                    act.wait_ge(S["turn"], n + 1)
                    wait_count(act, S["pv"], n - 1)
                    act.activation(probt[:, at[1] % 2, :], bank[(3, 6)[at[1] % 2]][:, :], ACT.Copy).then_inc(S["pt"], 1)
                tail.act_turn(act, ends(back(i, j, 8, per, outer)))
                tail.act_project(act, ends(back(i, j, 9, per, outer)))
            peeled(act, outer, per, step, 10)

        @block.vector
        def _(dve):
            dve.wait_ge(k.late[weights_of], k.late_count[weights_of])
            dve.memset(v[:, :, :, 8:9], 1.0)
            dve.tensor_scalar(k.negb[:, :], mask[:, :], mask_ops[0], mask_ops[1], mask_ops[2],
                              mask_ops[3]).then_inc(S["setup"], 1)
            dve.wait_ge(S["setup"], 1)

            def step(i, j):
                if (at := back(i, j, 2, per, outer)) and at[1] % CH == 0:
                    b, c = seq(*at), at[1] // CH
                    dve.wait_ge(S["projv"], b + 1)
                    wait_count(dve, S["pv"], (b - 1) * CH)
                    dve.tensor_tensor(v[:, c, :, 0:8],
                                      bank[0][:, 2 * P:3 * P].rearrange("p (h c) -> p h c", c=8),
                                      bv.rearrange("p (h c) -> p h c", c=8), ALU.add)\
                       .then_inc(S["v"], 1)
                if at := back(i, j, 4, per, outer):
                    n, b, m = at[0] * per + at[1], seq(*at), at[1] % 2
                    dve.wait_ge(S["score"], n + 1)
                    wait_count(dve, S["exp"], (n - 1) * 4)
                    dve.tensor_tensor(score[:, m, :, :],
                                      bank[1 + m][:, :].rearrange("p (h c) -> p h c", h=4),
                                      k.negb[:, bass.ds(b * P, P)].unsqueeze(1).broadcast_to([P, 4, P]),
                                      ALU.add).then_inc(S["mask"], 1)
                    dve.wait_ge(S["mask"], n + 1)
                    dve.tensor_reduce(nmax[:, m, :], score[:, m, :, :], AX.X, ALU.max, negate=True)\
                       .then_inc(S["max"], 1)
                if at := ends(back(i, j, 7, per, outer)):
                    b = seq(*at)
                    dve.wait_ge(S["pv"], (b + 1) * CH)
                    o = bank[4][:, 0:144].rearrange("p (h c) -> p h c", c=9)
                    dve.reciprocal(rinv.unsqueeze(2), o[:, :, 8:9]).then_inc(S["inv"], 1)
                    dve.wait_ge(S["inv"], b + 1)
                    wait_count(dve, S["tail1"], b)
                    dve.tensor_tensor(on.rearrange("p (h c) -> p h c", c=8), o[:, :, 0:8],
                                      rinv.unsqueeze(2).broadcast_to([P, 16, 8]), ALU.mult)\
                       .then_inc(S["on"], 1)
                tail.dve_add(dve, ends(back(i, j, 10, per, outer)))
            peeled(dve, outer, per, step, 11)



def wide_attention(k, tag, q_src, k_src, v_src, out_t=None):
    nc, bank, sub = k.nc, k.bank, 2
    a = Arena(k)
    vs = a.take(2 * P, "p (n c) -> p n c", n=2)
    qk = a.take(2 * 512, "p (n c) -> p n c", n=2)
    v = a.take(4 * 256, "p (n c) -> p n c", n=4)
    prob = a.take(2 * 512, "p (n h c) -> p n h c", n=2, h=4)
    probt = a.take(2 * 512, "p (n c) -> p n c", n=2)
    ot = a.take(2 * 256, "p (n c) -> p n c", n=2)
    nmax = a.take(8, "p (n h) -> p n h", n=2)
    rsum = a.take(8, "p (n h) -> p n h", n=2)
    rinv = a.take(8, "p (n h) -> p n h", n=2)
    yt = a.take(P)
    S = {n: k.sem(f"{tag}_" + n) for n in
         ("vs", "projqk", "projv", "qk", "v", "score", "max", "exp", "inv", "norm", "turn", "pt",
          "pv", "ot", "out", "done", "yt", "tail", "added", "stated")}
    wq, wk, wv, wo = (k.w[n] for n in ("wq1", "wk1", "wv1", "wo1"))
    CH = 4
    per, outer = 2 * CH, NB // 2

    def seq(i, j):
        return i * 2 + j // CH

    with nc.Block() as block:
        @block.tensor
        def _(pe):
            def step(i, j):
                if at := back(i, j, 0, per, outer):
                    n, b, c = at[0] * per + at[1], seq(*at), at[1] % CH
                    wait_count(pe, S["qk"], n)
                    for t in range(2):
                        w = slice((2 * c + t) * P, (2 * c + t + 1) * P)
                        pe.matmul(bank[0][:, t * P:(t + 1) * P], wq[:, w], q_src[:, bass.ds(b * P, P)],
                                  start=True, stop=True)
                        mm = pe.matmul(bank[0][:, (2 + t) * P:(3 + t) * P], wk[:, w],
                                       k_src[:, bass.ds(b * P, P)], start=True, stop=True)
                    mm.then_inc(S["projqk"], 1)
                    wait_count(pe, S["v"], n)
                    pe.wait_ge(S["vs"], b + 1)
                    pe.matmul(bank[1][:, 0:256], vs[:, at[1] // CH, :], wv[:, c * 256:(c + 1) * 256],
                              start=True, stop=True).then_inc(S["projv"], 1)
                if at := back(i, j, 1, per, outer):
                    n, m = at[0] * per + at[1], at[1] % 2
                    pe.wait_ge(S["qk"], n + 1)
                    wait_count(pe, S["exp"], n * 4)
                    for t in range(2):
                        for half in range(2):
                            r, c = 64 * half, t * P
                            mm = pe.matmul(bank[2 + half][:, c:c + P],
                                           qk[r:r + 64, m, t * P:(t + 1) * P],
                                           qk[r:r + 64, m, (2 + t) * P:(3 + t) * P],
                                           start=True, stop=True)
                    mm.then_inc(S["score"], 1)
                if at := back(i, j, 2, per, outer):
                    n, m = at[0] * per + at[1], at[1] % 2
                    pe.wait_ge(S["norm"], n + 1)
                    wait_count(pe, S["pt"], n)
                    for h in range(4):
                        mm = pe.transpose(bank[4][:, h * P:(h + 1) * P], prob[:, m, h, :],
                                          k.ident[:, :])
                    mm.then_inc(S["turn"], 1)
                if at := back(i, j, 3, per, outer):
                    n, m = at[0] * per + at[1], at[1] % 2
                    pe.wait_ge(S["pt"], n + 1)
                    pe.wait_ge(S["v"], n + 1)
                    wait_count(pe, S["ot"], n)
                    for t in range(2):
                        for half in range(2):
                            h, slot = 2 * t + half, 2 * half + t
                            mm = pe.matmul(bank[6][64 * half:64 * half + 64, t * P:(t + 1) * P],
                                           v[:, at[1] % 4, h * 64:(h + 1) * 64],
                                           probt[:, m, slot * P:(slot + 1) * P], start=True, stop=True)
                    mm.then_inc(S["pv"], 1)
                if at := back(i, j, 4, per, outer):
                    n, b, c, m = at[0] * per + at[1], seq(*at), at[1] % CH, at[1] % 2
                    pe.wait_ge(S["ot"], n + 1)
                    if c == 0:
                        wait_count(pe, S["yt" if out_t is None else "done"], b)
                    for t in range(2):
                        w = slice((2 * c + t) * P, (2 * c + t + 1) * P)
                        mm = pe.matmul(bank[7][:, 0:P], wo[:, w], ot[:, m, t * P:(t + 1) * P],
                                       start=(c == 0 and t == 0), stop=(c == CH - 1 and t == 1))
                    mm.then_inc(S["out"], 1)
                if out_t is None and (at := back(i, j, 5, per, outer)) and at[1] % CH == CH - 1:
                    b = seq(*at)
                    pe.wait_ge(S["yt"], b + 1)
                    wait_count(pe, S["added"], b)
                    pe.transpose(bank[5][:, 0:P], yt, k.ident[:, :]).then_inc(S["tail"], 1)
            peeled(pe, outer, per, step, 6)

        @block.gpsimd
        def _(pool):
            def step(i, j):
                if j % CH == 0:
                    b, c = seq(i, j), j // CH
                    wait_count(pool, S["projv"], (b - 1) * CH)
                    pool.tensor_copy(vs[:, c, :], v_src[:, bass.ds(b * P, P)]).then_inc(S["vs"], 1)
            peeled(pool, outer, per, step, 0)

        @block.scalar
        def _(act):
            def step(i, j):
                if at := back(i, j, 0, per, outer):
                    n = at[0] * per + at[1]
                    act.wait_ge(S["projv"], n + 1)
                    wait_count(act, S["pv"], n - 3)
                    act.activation(v[:, at[1] % 4, :], bank[1][:, 0:256], ACT.Copy).then_inc(S["v"], 1)
                if at := back(i, j, 2, per, outer):
                    n, m = at[0] * per + at[1], at[1] % 2
                    act.wait_ge(S["turn"], n + 1)
                    wait_count(act, S["pv"], n - 1)
                    act.activation(probt[:, m, :], bank[4][:, :], ACT.Copy).then_inc(S["pt"], 1)
                if at := back(i, j, 1, per, outer):
                    n, m = at[0] * per + at[1], at[1] % 2
                    act.wait_ge(S["max"], n + 1)
                    wait_count(act, S["turn"], n - 1)
                    for h in range(4):
                        c = (h % 2) * P
                        act.activation(prob[:, m, h, :], bank[2 + h // 2][:, c:c + P], ACT.Exp,
                                       bias=nmax[:, m, h:h + 1],
                                       accum_out=rsum[:, m, h:h + 1]).then_inc(S["exp"], 1)
                if out_t is None and (at := back(i, j, 4, per, outer)) and at[1] % CH == CH - 1:
                    b = seq(*at)
                    act.wait_ge(S["out"], (b + 1) * CH)
                    wait_count(act, S["tail"], b)
                    act.activation(yt, bank[7][:, 0:P], ACT.Identity, scale=k.gate[:, sub:sub + 1],
                                   bias=k.gbias[:, sub:sub + 1]).then_inc(S["yt"], 1)
            peeled(act, outer, per, step, 5)

        @block.vector
        def _(dve):
            def step(i, j):
                if at := back(i, j, 0, per, outer):
                    n, m = at[0] * per + at[1], at[1] % 2
                    dve.wait_ge(S["projqk"], n + 1)
                    wait_count(dve, S["score"], n - 1)
                    dve.tensor_copy(qk[:, m, :], bank[0][:, :]).then_inc(S["qk"], 1)
                if at := back(i, j, 1, per, outer):
                    n, m = at[0] * per + at[1], at[1] % 2
                    dve.wait_ge(S["score"], n + 1)
                    wait_count(dve, S["exp"], (n - 1) * 4)
                    dve.tensor_reduce(nmax[:, m, :].rearrange("p (half t) -> p half t", half=2),
                                      k.psum[:, 2:4, 0:256]
                                      .rearrange("p half (t c) -> p half t c", t=2),
                                      AX.X, ALU.max, negate=True).then_inc(S["max"], 1)
                if at := back(i, j, 3, per, outer):
                    n, m = at[0] * per + at[1], at[1] % 2
                    dve.wait_ge(S["pv"], n + 1)
                    wait_count(dve, S["out"], n - 1)
                    dve.tensor_copy(ot[:, m, :], bank[6][:, 0:256]).then_inc(S["ot"], 1)
                if at := back(i, j, 1, per, outer):
                    n, m = at[0] * per + at[1], at[1] % 2
                    dve.wait_ge(S["exp"], (n + 1) * 4)
                    dve.reciprocal(rinv[:, m, :], rsum[:, m, :]).then_inc(S["inv"], 1)
                    dve.wait_ge(S["inv"], n + 1)
                    dve.tensor_tensor(prob[:, m, :, :], prob[:, m, :, :],
                                      rinv[:, m, :].unsqueeze(2).broadcast_to([P, 4, P]), ALU.mult)\
                       .then_inc(S["norm"], 1)
                if (at := back(i, j, 4, per, outer)) and at[1] % CH == CH - 1 and out_t is not None:
                    b = seq(*at)
                    dve.wait_ge(S["out"], (b + 1) * CH)
                    dve.scalar_tensor_tensor(out=out_t[:, bass.ds(b * P, P)], in0=bank[7][:, 0:P],
                                             scalar=k.col("bo1"), in1=k.xnt[:, bass.ds(b * P, P)],
                                             op0=ALU.add, op1=ALU.add).then_inc(S["done"], 1)
                if (at := back(i, j, 5, per, outer)) and at[1] % CH == CH - 1 and out_t is None:
                    b = seq(*at)
                    dve.wait_ge(S["tail"], b + 1)
                    residual(k, dve, sub, b, bank[5][:, 0:P], S["added"], S["stated"], 0, b)
            peeled(dve, outer, per, step, 6)



def feed_forward(k, tag, sub, tiles, function, one_down=False):
    nc, bank = k.nc, k.bank
    J = len(tiles)
    a = Arena(k)
    h1 = a.take(2 * GT, "p (n c) -> p n c", n=2)
    h2 = a.take(2 * GT, "p (n c) -> p n c", n=2)
    h3 = a.take(2 * GT, "p (n c) -> p n c", n=2)
    yt = a.take(GT)
    total = a.take(2 * GT, "p (n c) -> p n c", n=2)
    new, bn, mean_var = a.take(GT), a.take(6 * GB, "p (b c) -> p b c", b=GB), a.take(2 * GB)
    S = {n: k.sem(f"{tag}_" + n) for n in
         ("up", "act", "summed", "second", "made_dve", "made_act", "down", "yt", "tail", "added", "stated", "stored")}
    second = tiles[0][2] is not None
    last_sub = sub == 7

    by_dve = [t[2] is not None or t[3] is not None for t in tiles]
    NV = sum(by_dve)

    def free(j):
        return 2 if j >= 2 or J % 2 == 0 else (1, 3)[j]

    def wait_hidden(eng, g, j):
        if by_dve[j]:
            eng.wait_ge(S["made_dve"], g * NV + sum(by_dve[:j + 1]))
        else:
            eng.wait_ge(S["made_act"], g * (J - NV) + j + 1 - sum(by_dve[:j + 1]))

    def wait_last_hidden(eng, at):
        if before := back(*at, free(at[1]), J, NG):
            wait_hidden(eng, *before)

    with nc.Block() as block:
        @block.tensor
        def _(pe):
            def step(i, j):
                if at := back(i, j, 0, J, NG):
                    n, m = at[0] * J + at[1], at[1] % 2
                    up, _, sec, sel, _ = tiles[at[1]]
                    group = bass.ds(at[0] * GT, GT)
                    wait_last_hidden(pe, at)
                    mm = pe.matmul(bank[m][:, :], up, k.xnt[:, group], start=True, stop=True)
                    if sec is not None:
                        mm = pe.matmul(bank[2 + m][:, :], sec, k.xnt[:, group], start=True, stop=True)
                    if sel is not None:
                        mm = pe.matmul(bank[4 + m][:, :], sel, k.combt[:, group], start=True, stop=True)
                    mm.then_inc(S["up"], 1)
                if one_down and (at := back(i, j, 2, J, NG)) and at[1] == J - 1:
                    pe.wait_ge(S["summed"], (at[0] + 1) * (J - 1))
                    wait_count(pe, S["yt"], at[0])
                    pe.matmul(bank[6][:, :], tiles[0][4], total[:, (J - 1) % 2, :], start=True,
                              stop=True).then_inc(S["down"], 1)
                if not one_down and (at := back(i, j, 2, J, NG)):
                    n, m = at[0] * J + at[1], at[1] % 2
                    wait_hidden(pe, *at)
                    if at[1] == 0:
                        wait_count(pe, S["yt"], at[0])
                    pe.matmul(bank[6][:, :], tiles[at[1]][4], h3[:, m, :], start=(at[1] == 0),
                              stop=(at[1] == J - 1)).then_inc(S["down"], 1)
                if (at := back(i, j, 3, J, NG)) and at[1] == J - 1:
                    pe.wait_ge(S["yt"], at[0] + 1)
                    wait_count(pe, S["added"], at[0])
                    for b in range(GB):
                        mm = pe.transpose(bank[7][:, b * P:(b + 1) * P], yt[:, b * P:(b + 1) * P],
                                          k.ident[:, :])
                    mm.then_inc(S["tail"], 1)
            peeled(pe, NG, J, step, 3)

        @block.scalar
        def _(act):
            def step(i, j):
                if (at := back(i, j, 2, J, NG)) and at[1] == J - 1:
                    act.wait_ge(S["down"], (at[0] + 1) * (1 if one_down else J))
                    wait_count(act, S["tail"], at[0])
                    act.activation(yt, bank[6][:, :], ACT.Identity, scale=k.gate[:, sub:sub + 1],
                                   bias=k.gbias[:, sub:sub + 1]).then_inc(S["yt"], 1)
                if at := back(i, j, 0, J, NG):
                    n, m = at[0] * J + at[1], at[1] % 2
                    _, bias, _, sel, _ = tiles[at[1]]
                    act.wait_ge(S["up"], n + 1)
                    if by_dve[at[1]]:
                        wait_last_hidden(act, at)
                        act.activation(h1[:, m, :], bank[m][:, :], function,
                                       bias=bias if bias is not None else 0.0).then_inc(S["act"], 1)
                    else:
                        wait_count(act, S["down"], n + 1 - free(at[1]))
                        act.activation(h3[:, m, :], bank[m][:, :], function,
                                       bias=bias if bias is not None else 0.0)\
                           .then_inc(S["made_act"], 1)
            peeled(act, NG, J, step, 3)

        @block.vector
        def _(dve):
            experts = sum(t[3] is not None for t in tiles)

            def step(i, j):
                if at := back(i, j, 0, J, NG):
                    g, t = at
                    n, m = g * J + t, t % 2
                    _, _, sec, sel, _ = tiles[t]
                    if one_down:
                        dve.wait_ge(S["act"], n + 1)
                        dst = h2[:, 0, :] if t == 0 else h3[:, m, :]
                        if t == 1:
                            wait_count(dve, S["summed"], g * (J - 1))
                        if t >= 3:
                            dve.wait_ge(S["summed"], g * (J - 1) + t - 2)
                        dve.tensor_tensor(dst, bank[4 + m][:, :], h1[:, m, :], ALU.mult)\
                           .then_inc(S["made_dve"], 1)
                    elif by_dve[t]:
                        dve.wait_ge(S["act"], g * NV + sum(by_dve[:t + 1]))
                        wait_count(dve, S["down"], n + 1 - free(t))
                        if second and sel is not None:
                            dve.tensor_tensor(h2[:, m, :], bank[2 + m][:, :], h1[:, m, :], ALU.mult)\
                               .then_inc(S["second"], 1)
                            dve.wait_ge(S["second"], g * experts + t + 1)
                            dve.tensor_tensor(h3[:, m, :], bank[4 + m][:, :], h2[:, m, :], ALU.mult)\
                               .then_inc(S["made_dve"], 1)
                        else:
                            src = bank[4 + m] if sel is not None else bank[2 + m]
                            dve.tensor_tensor(h3[:, m, :], src[:, :], h1[:, m, :], ALU.mult)\
                               .then_inc(S["made_dve"], 1)
                if one_down and (at := back(i, j, 1, J, NG)) and at[1] >= 1:
                    g, t = at
                    dve.wait_ge(S["made_dve"], g * J + t + 1)
                    if t >= 2:
                        dve.wait_ge(S["summed"], g * (J - 1) + t - 1)
                    if t % 2 == (J - 1) % 2:
                        wait_count(dve, S["down"], g)
                    before = h2[:, 0, :] if t == 1 else total[:, (t - 1) % 2, :]
                    dve.tensor_tensor(total[:, t % 2, :], before, h3[:, t % 2, :], ALU.add)\
                       .then_inc(S["summed"], 1)
                if (at := back(i, j, 3, J, NG)) and at[1] == J - 1:
                    g = at[0]
                    dve.wait_ge(S["tail"], g + 1)
                    xg = k.x[:, bass.ds(g * GT, GT)]
                    if last_sub:
                        dve.tensor_tensor(xg, bank[7][:, :], xg, ALU.add).then_inc(S["added"], 1)
                    else:
                        dve.tensor_tensor(new, bank[7][:, :], xg, ALU.add).then_inc(S["added"], 1)
                        dve.wait_ge(S["added"], g + 1)
                        for b in range(GB):
                            ins = dve.bn_stats(bn[:, b, :], new[:, b * P:(b + 1) * P])
                        ins.then_inc(S["stated"], 1)
                        dve.wait_ge(S["stated"], 2 * g + 1)
                        dve.tensor_scalar(xg, new, 1.0, None, ALU.mult)
                        for b in range(GB):
                            ins = dve.bn_aggr(mean_var[:, 2 * b:2 * b + 2], bn[:, b, :])
                        ins.then_inc(S["stated"], 1)
                        dve.wait_ge(S["stated"], 2 * g + 2)
                        dve.tensor_scalar(k.mv[:, bass.ds(g * (2 * GB), 2 * GB)], mean_var, 1.0, None,
                                          ALU.mult)
            peeled(dve, NG, J, step, 4 if J >= 4 else 3)

        if last_sub:
            @block.sync
            def _(sp):
                for g in range(NG):
                    sp.wait_ge(S["added"], g + 1)
                    sp.dma_start(k.out[:, g * GT:(g + 1) * GT], k.x[:, g * GT:(g + 1) * GT])\
                      .then_inc(S["stored"], 16)
                sp.wait_ge(S["stored"], 16 * NG)


def make_selectors(pool, k, experts, width, sem, n):
    s = k.sels[:, 0:experts * width].rearrange("p (e c) -> p e c", c=width)
    pool.memset(k.sels[:, 0:experts * width], 0.0).then_inc(sem, 1)
    for part in range(3):
        pool.wait_ge(sem, n + part + 1)
        pool.affine_select(out=s, in_=s, compare_op=ALU.not_equal, fill=1.0, base=-part * experts,
                           pattern=[[-1, experts], [0, width]], channel_multiplier=1).then_inc(sem, 1)


def route(k, tag, E, groups, top_groups, top, kind, gate_w, rbias=None, factor=1.0, width=64,
          weights_of=0):
    nc, bank = k.nc, k.bank
    a = Arena(k)
    st = a.take(T)
    TE = NB * E

    def take():
        return a.take(TE, "p (t e) -> p t e", t=NB)

    s, v, rank, cmp, sel, w = take(), take(), take(), take(), take(), take()
    G = groups or 1
    gs = E // G
    gsc, grank, gcmp = (a.take(NB * G, "p (t g) -> p t g", t=NB) for _ in range(3))
    tmp = [a.take(NB * G, "p (t g) -> p t g", t=NB) for _ in range(4)]
    tot, parts = a.take(NB), a.take(3 * TE, "p (t q e) -> p t q e", t=NB, q=3)
    low = a.take(TE, "p (t e) -> p t e", t=NB)
    best = a.take(NB * 8, "p (t e) -> p t e", t=NB)
    bf = k.big[2][:, 0:(TE + 1) // 2].bitcast(BF16).rearrange("p (t e) -> p t e", t=NB)
    S = {n: k.sem(f"{tag}_" + n) for n in
         ("logit", "st", "turn", "chain", "exp", "parts", "turn2", "comb", "sel")}

    with nc.Block() as block:
        @block.tensor
        def _(pe):
            pe.wait_ge(k.late[weights_of], k.late_count[weights_of])
            for g in range(NG):
                pe.matmul(bank[g][0:E, :], gate_w, k.xnt[:, g * GT:(g + 1) * GT],
                          start=True, stop=True).then_inc(S["logit"], 1)
            for b in range(NB):
                if b % GB == 0:
                    pe.wait_ge(S["st"], b // GB + 1)
                mm = pe.transpose(bank[4][:, b * E:(b + 1) * E], st[0:E, b * P:(b + 1) * P],
                                  k.ident[0:E, 0:E])
            mm.then_inc(S["turn"], 1)
            pe.wait_ge(S["parts"], 1)
            for b in range(NB):
                mm = pe.transpose(bank[b // GB][0:3 * E, (b % GB) * P:(b % GB + 1) * P],
                                  parts[:, b, :, :].rearrange("p q e -> p (q e)"), k.ident[:, :])
                if b % GB == GB - 1:
                    mm.then_inc(S["turn2"], 1)

        @block.scalar
        def _(act):
            for g in range(NG):
                act.wait_ge(S["logit"], g + 1)
                act.activation(st[0:E, g * GT:(g + 1) * GT], bank[g][0:E, :],
                               ACT.Sigmoid if kind == "sigmoid" else ACT.Copy).then_inc(S["st"], 1)
            if kind == "softmax":
                act.wait_ge(S["chain"], 2)
                act.activation(v, s, ACT.Exp).then_inc(S["exp"], 1)
            act.wait_ge(S["sel"], 5)
            for g in range(NG):
                act.wait_ge(S["turn2"], g + 1)
                act.activation(k.combt[0:3 * E, g * GT:(g + 1) * GT], bank[g][0:3 * E, :], ACT.Copy)\
                   .then_inc(S["comb"], 1)

        @block.gpsimd
        def _(pool):
            pool.memset(k.combt[:, :], 0.0).then_inc(S["sel"], 1)
            make_selectors(pool, k, E, width, S["sel"], 1)

        @block.vector
        def _(dve):
            done = [0]

            def link(ins):
                done[0] += 1
                ins.then_inc(S["chain"], 1)
                dve.wait_ge(S["chain"], done[0])

            def ranks(val, r, c, n, span):
                for e in range(span):
                    ins = dve.memset(r[:, :, e::span] if span < n else r[:, :, e:e + 1],
                                     float(span - 1 - e))
                link(ins)
                vv = val.rearrange("p t (g s) -> p (t g) s", s=span)
                rr = r.rearrange("p t (g s) -> p (t g) s", s=span)
                cc = c.rearrange("p t (g s) -> p (t g) s", s=span)
                for o in range(1, span):
                    link(dve.tensor_tensor(cc[:, :, 0:span - o], vv[:, :, 0:span - o], vv[:, :, o:span],
                                           ALU.is_ge))
                    link(dve.tensor_tensor(rr[:, :, 0:span - o], rr[:, :, 0:span - o],
                                           cc[:, :, 0:span - o], ALU.subtract))
                    link(dve.tensor_tensor(rr[:, :, o:span], rr[:, :, o:span], cc[:, :, 0:span - o],
                                           ALU.add))

            def choose(chosen, val, n, count, same, spare):
                for b in range(NB):
                    ins = dve.max(best[:, b, :], val[:, b, :])
                link(ins)
                edge = best[:, :, count - 1:count].broadcast_to([P, NB, n])
                dve.tensor_tensor(chosen, val, edge, ALU.is_gt)
                link(dve.tensor_tensor(same, val, edge, ALU.is_equal))
                link(dve.tensor_reduce(tot, chosen, AX.X, ALU.add))
                link(dve.tensor_scalar(tot, tot, -1.0, float(count), ALU.mult, ALU.add))
                src, o = same, 1
                while o < n:
                    dst = spare[0]
                    dve.tensor_scalar(dst[:, :, 0:o], src[:, :, 0:o], 1.0, None, ALU.mult)
                    link(dve.tensor_tensor(dst[:, :, o:n], src[:, :, o:n], src[:, :, 0:n - o], ALU.add))
                    src, o, spare = dst, 2 * o, spare[::-1]
                link(dve.tensor_tensor(src, src, tot.unsqueeze(2).broadcast_to([P, NB, n]), ALU.is_le))
                link(dve.tensor_tensor(src, src, same, ALU.mult))
                link(dve.tensor_tensor(chosen, chosen, src, ALU.add))

            dve.wait_ge(S["turn"], 1)
            p_s = bank[4][:, 0:TE].rearrange("p (t e) -> p t e", t=NB)
            if kind == "softmax":
                link(dve.tensor_reduce(tot, p_s, AX.X, ALU.max))
                link(dve.tensor_tensor(s, p_s, tot.unsqueeze(2).broadcast_to([P, NB, E]), ALU.subtract))
                dve.wait_ge(S["exp"], 1)
                link(dve.tensor_reduce(tot, v, AX.X, ALU.add))
                link(dve.reciprocal(tot, tot))
                link(dve.tensor_tensor(s, v, tot.unsqueeze(2).broadcast_to([P, NB, E]), ALU.mult))
                choose(sel, s, E, top, cmp, (rank, low))
            else:
                link(dve.tensor_copy(s, p_s))
                base = s
                if rbias is not None:
                    link(dve.tensor_tensor(w, s, rbias.unsqueeze(1).broadcast_to([P, NB, E]), ALU.add))
                    base = w
                if rbias is not None:
                    link(dve.tensor_reduce(gsc, base.rearrange("p t (g s) -> p t g s", s=gs), AX.X,
                                           ALU.max))
                else:
                    q = base.rearrange("p t (g s) -> p t g s", s=gs)
                    hi1, lo1, hi2, lo2 = tmp
                    dve.tensor_tensor(hi1, q[:, :, :, 0], q[:, :, :, 1], ALU.max)
                    dve.tensor_tensor(lo1, q[:, :, :, 0], q[:, :, :, 1], ALU.min)
                    dve.tensor_tensor(hi2, q[:, :, :, 2], q[:, :, :, 3], ALU.max)
                    link(dve.tensor_tensor(lo2, q[:, :, :, 2], q[:, :, :, 3], ALU.min))
                    link(dve.tensor_tensor(gsc, hi1, hi2, ALU.max))
                    link(dve.tensor_tensor(hi1, hi1, hi2, ALU.min))
                    link(dve.tensor_tensor(lo1, lo1, lo2, ALU.max))
                    link(dve.tensor_tensor(hi1, hi1, lo1, ALU.max))
                    link(dve.tensor_tensor(gsc, gsc, hi1, ALU.add))
                if G >= 8:
                    choose(gcmp, gsc, G, top_groups, grank, tmp[0:2])
                else:
                    ranks(gsc, grank, gcmp, G, G)
                    link(dve.tensor_scalar(gcmp, grank, float(top_groups), None, ALU.is_lt))
                link(dve.tensor_tensor(v.rearrange("p t (g s) -> p t g s", s=gs),
                                       base.rearrange("p t (g s) -> p t g s", s=gs),
                                       gcmp.unsqueeze(3).broadcast_to([P, NB, G, gs]), ALU.mult))
                choose(sel, v, E, top, cmp, (rank, low))
            link(dve.tensor_tensor(w, s, sel, ALU.mult))
            if kind == "sigmoid":
                link(dve.tensor_reduce(tot, w, AX.X, ALU.add))
                link(dve.tensor_scalar(tot, tot, 1e-20, None, ALU.add))
                link(dve.reciprocal(tot, tot))
                link(dve.tensor_scalar(tot, tot, factor, None, ALU.mult))
                link(dve.tensor_tensor(w, w, tot.unsqueeze(2).broadcast_to([P, NB, E]), ALU.mult))
            link(dve.tensor_copy(bf, w))
            link(dve.tensor_copy(parts[:, :, 0, :], bf))
            link(dve.tensor_tensor(low, w, parts[:, :, 0, :], ALU.subtract))
            link(dve.tensor_copy(bf, low))
            link(dve.tensor_copy(parts[:, :, 1, :], bf))
            dve.tensor_tensor(parts[:, :, 2, :], low, parts[:, :, 1, :], ALU.subtract)\
               .then_inc(S["parts"], 1)


def prepare_l1(k):
    nc, bank = k.nc, k.bank
    a = Arena(k)
    peak, allpeak, per_step, step_size, spread = (a.take(2) for _ in range(5))
    ones, turned_max = a.take(P), a.take(2)[0:2, 0:1]
    q = [a.take(512), a.take(512)]
    chain, peaked, reduced, lora = (k.sem("l1w_" + n) for n in ("chain", "peak", "reduced", "lora"))
    wfc, wproj = k.w["wfc"], k.w["wproj"]
    with nc.Block() as block:
        @block.vector
        def _(dve):
            done = [0]

            def link(ins):
                done[0] += 1
                ins.then_inc(chain, 1)
                dve.wait_ge(chain, done[0])

            dve.wait_ge(k.late[1], k.late_count[1])
            link(dve.tensor_scalar(k.w["wq1"][:, :], k.w["wq1"][:, :], 0.125, None, ALU.mult))
            dve.memset(ones, 1.0)
            for n, w in enumerate((wfc, wproj)):
                dve.tensor_reduce(peak[:, n:n + 1], w[:, :], AX.X, ALU.max, apply_absolute_value=True)\
                   .then_inc(peaked, 1)
            dve.wait_ge(reduced, 1)
            link(dve.tensor_reduce(turned_max, bank[2][0:2, 0:P], AX.X, ALU.max))
            dve.tensor_scalar(spread[0:2, :], k.ident[0:2, 0:2], turned_max, None, ALU.mult)\
               .then_inc(peaked, 1)
            dve.wait_ge(reduced, 2)
            link(dve.tensor_copy(allpeak, bank[3][:, 0:2]))
            link(dve.tensor_scalar(step_size, allpeak, 1.0 / 127.0, None, ALU.mult))
            link(dve.reciprocal(per_step, step_size))
            for n, w in enumerate((wfc, wproj)):
                link(dve.tensor_scalar(q[n], w[:, :], per_step[:, n:n + 1], None, ALU.mult))
                link(dve.tensor_scalar(q[n], q[n], ROUND, ROUND, ALU.add, ALU.subtract))
                link(dve.tensor_scalar(q[n], q[n], -128.0, 127.0, ALU.max, ALU.min))
                link(dve.scalar_tensor_tensor(out=q[n], in0=q[n], scalar=step_size[:, n:n + 1],
                                              in1=w[:, :], op0=ALU.mult, op1=ALU.subtract))
                link(dve.tensor_tensor(w[:, :], w[:, :], q[n], ALU.add))
            dve.wait_ge(lora, 1)
            for n, w in enumerate((wfc, wproj)):
                link(dve.scalar_tensor_tensor(out=w[:, :], in0=bank[n][:, :], scalar=2.0, in1=w[:, :],
                                              op0=ALU.mult, op1=ALU.add))

        @block.tensor
        def _(pe):
            pe.wait_ge(k.late[1], k.late_count[1])
            pe.matmul(bank[0][:, :], k.w["afc"][:, :], k.w["bfct"][:, :], start=True, stop=True)
            for t in range(4):
                mm = pe.matmul(bank[1][:, t * P:(t + 1) * P], k.w["aproj"][:, t * P:(t + 1) * P],
                               k.w["bprojt"][:, :], start=True, stop=True)
            mm.then_inc(lora, 1)
            pe.wait_ge(peaked, 2)
            pe.transpose(bank[2][0:2, 0:P], peak, k.ident[:, :]).then_inc(reduced, 1)
            pe.wait_ge(peaked, 3)
            pe.matmul(bank[3][:, 0:2], ones[0:2, :], spread[0:2, :], start=True, stop=True)\
              .then_inc(reduced, 1)


def build(nc, dram, out, stages=8):
    ctx = ExitStack()
    with ctx:
        k = Kernel(nc, ctx, dram, out)
        w = k.w
        load_and_constants(k)

        def cut(name, n, width=P):
            return w[name][:, n * width:(n + 1) * width]

        ctxn, lat = k.combined = (k.big[2], k.xnt)
        v0 = k.work[:, 13 * 1024 - 2 * T:].rearrange("p (s c) -> p s c", s=2)
        k.stage(normalise, "n_ctx", k.ctx_tok, k.ctx_tok, ctxn, k.col("ln_x_g"), k.col("ln_x_b"), stats=True)
        k.stage(normalise, "n_lat", k.x, k.xn, lat, k.col("ln_l_g"), k.col("ln_l_b"), stats=True,
                twice=True)
        qn, kl, kc = k.big[0], k.big[1], k.ctx_tok
        k.stage(l0_queries_keys_values, lat, ctxn, qn, kl, kc, v0)
        k.stage(l0_attention, qn, kl, kc, v0)
        if stages > 1:
            k.stage(normalise, "n1", k.x, k.xn, k.xnt)
            k.stage(route, "r0", 16, 4, 2, 4, "sigmoid", w["gate0"][:, :], factor=2.5, width=64)
            tiles = [(cut("up0", j), None, None, k.sels[:, j * P:(j + 1) * P], cut("down0", j))
                     for j in range(8)]
            tiles += [(cut("sup0", j), None, None, None, cut("sdown0", j)) for j in range(2)]
            k.stage(feed_forward, "f0", 1, tiles, ACT.Silu)
        g3u3 = [(w["g3"], dram["g3"]), (w["u3"], dram["u3"])]
        if stages > 2:
            k.stage(prepare_l1)
            k.stage(normalise, "n2", k.x, k.xn, k.xnt, loads=g3u3)
            k.stage(wide_attention, "a1", k.xnt, k.ctxt, k.ctxt, k.big[0])
            k.stage(wide_attention, "b1", k.big[0], k.big[0], k.xnt)
        if stages > 3:
            k.stage(normalise, "n3", k.x, k.xn, k.xnt)
            tiles = [(cut("wfc", j), k.cols[:, C_BFC + j:C_BFC + j + 1], None, None, cut("wproj", j))
                     for j in range(4)]
            k.stage(feed_forward, "f1", 3, tiles, ACT.Gelu)
        if stages > 4:
            k.stage(normalise, "n4", k.x, k.xn, k.xnt)
            k.stage(small_head_attention, "a2", 4, ("wq2", "wk2", "wv2", "wo2"), k.col("bq2"), k.col("bk2"),
                                 k.rows[:, R_BV2:R_BV2 + P], k.mask2,
                                 (0.0, MASKED, ALU.is_equal, ALU.mult), 2)
        if stages > 5:
            k.stage(normalise, "n5", k.x, k.xn, k.xnt,
                    loads=[(k.mask3, dram["mask3"].broadcast_to([P, T]))])
            k.stage(route, "r2", 8, None, None, 2, "softmax", w["gate2"][:, :], width=128, weights_of=2)
            tiles = [(cut("ew2", j), k.cols[:, C_EB + j:C_EB + j + 1], None,
                      k.sels[:, j * P:(j + 1) * P], w["comb2"][:, :]) for j in range(8)]
            k.stage(feed_forward, "f2", 5, tiles, ACT.Silu, one_down=True)
        if stages > 6:
            k.stage(normalise, "n6", k.x, k.xn, k.xnt)
            k.stage(small_head_attention, "a3", 6, ("wq3", "wk3", "wv3", "wo3"), k.col("bq3"), k.col("bk3"),
                                 k.rows[:, R_BV3:R_BV3 + P], k.mask3,
                                 (-1e9, None, ALU.mult, ALU.bypass), 3)
        if stages > 7:
            k.stage(normalise, "n7", k.x, k.xn, k.xnt)
            k.stage(route, "r3", 32, 8, 4, 6, "sigmoid", w["gate3"][:, :],
                  rbias=k.rows[:, R_SB:R_SB + 32], factor=2.5, width=64, weights_of=3)
            tiles = [(cut("g3", j), None, cut("u3", j), k.sels[:, j * P:(j + 1) * P], cut("down3", j))
                     for j in range(16)]
            tiles += [(w["sg3"][:, :], None, w["su3"][:, :], None, w["sd3"][:, :])]
            k.stage(feed_forward, "f3", 7, tiles, ACT.Silu)
        else:
            stored = k.sem("stored")
            with nc.Block() as block:
                @block.sync
                def _(sp):
                    sp.dma_start(out, k.x[:, :]).then_inc(stored, 16)
                    sp.wait_ge(stored, 16)


def layout(i):
    import numpy as np
    a = {n: np.asarray(v) for n, v in i.items()}

    def t(x):
        return np.ascontiguousarray(x.T)

    def tiles(x):
        n = x.shape[0] // P
        return np.ascontiguousarray(x.reshape(n, P, -1).transpose(1, 0, 2).reshape(P, -1))

    def tok(x):
        return tiles(x.reshape(T, P))

    d = {
        "x": tok(a["x"]), "ctx": tok(a["ctx_1024"]), "ctxt": t(a["ctx_1024"].reshape(T, P)),
        "mask0": a["mask_BxS2_bk0"].reshape(1, T),
        "mask2": np.ascontiguousarray(a["mask_Bx1xSxS2_ik1"].reshape(NB, P, P).transpose(1, 0, 2).reshape(P, T)),
        "mask3": np.ascontiguousarray(a["mask_Bx1x1xS2_ik0"].reshape(1, T)),
        "wq0": a["L0_xattn_W_q"], "wkv0": a["L0_xattn_W_kv"], "wo0": a["L0_xattn_W_out"],
        "gate0": t(a["L0_ffn_gate_weight"]),
        "up0": np.ascontiguousarray(a["L0_ffn_expert_up"].transpose(1, 0, 2).reshape(P, 1024)),
        "down0": tiles(a["L0_ffn_expert_down"].reshape(1024, P)),
        "sup0": a["L0_ffn_shared_up"], "sdown0": tiles(a["L0_ffn_shared_down"]),
        "wq1": a["L1_xattn_Wq"], "wk1": a["L1_xattn_Wk"], "wv1": a["L1_xattn_Wv"],
        "wo1": tiles(a["L1_xattn_Wo"]),
        "wfc": t(a["L1_ffn_W_fc"]), "wproj": tiles(t(a["L1_ffn_W_proj"])),
        "afc": a["L1_ffn_A_fc"], "bfct": t(a["L1_ffn_B_fc"]),
        "aproj": a["L1_ffn_A_proj"], "bprojt": t(a["L1_ffn_B_proj"]),
        "wq2": a["L2_xattn_Wq"], "wk2": a["L2_xattn_Wk"], "wv2": a["L2_xattn_Wv"], "wo2": a["L2_xattn_Wo"],
        "gate2": t(a["L2_ffn_gate_w"]),
        "ew2": np.ascontiguousarray(a["L2_ffn_expert_w"].transpose(2, 0, 1).reshape(P, 1024)),
        "comb2": t(a["L2_ffn_combine_w"]),
        "wq3": a["L3_xattn_wq"], "wk3": a["L3_xattn_wk"], "wv3": a["L3_xattn_wv"], "wo3": a["L3_xattn_wo"],
        "gate3": t(a["L3_ffn_gate_weight"]),
        "g3": np.ascontiguousarray(a["L3_ffn_experts_gate_up"][:, :64].transpose(2, 0, 1).reshape(P, 2048)),
        "u3": np.ascontiguousarray(a["L3_ffn_experts_gate_up"][:, 64:].transpose(2, 0, 1).reshape(P, 2048)),
        "down3": tiles(np.ascontiguousarray(a["L3_ffn_experts_down"].transpose(0, 2, 1)).reshape(2048, P)),
        "sg3": t(a["L3_ffn_shared_gate_w"]), "su3": t(a["L3_ffn_shared_up_w"]),
        "sd3": t(a["L3_ffn_shared_down_w"]),
    }
    cols = [a["L0_xattn_ln_x_g"], a["L0_xattn_ln_x_b"], a["L0_xattn_ln_l_g"], a["L0_xattn_ln_l_b"],
            np.concatenate([a["L0_xattn_q_gamma"]] * 2), np.concatenate([a["L0_xattn_k_gamma"]] * 2),
            a["L0_xattn_b_out"], a["L1_xattn_bo"], a["L1_ffn_b_proj"],
            a["L2_xattn_bq"], a["L2_xattn_bk"], a["L2_xattn_bo"],
            a["L3_xattn_bq"], a["L3_xattn_bk"], a["L3_xattn_bo"]]
    cols += list(a["L1_ffn_b_fc"].reshape(4, P)) + list(a["L2_ffn_expert_b"])
    d["cols"] = np.ascontiguousarray(np.stack(cols, axis=1))
    gates = np.stack([a["g_xattn"], a["g_ffn"]], axis=1).reshape(8)
    row = np.concatenate([gates, a["L2_xattn_bv"], a["L3_xattn_bv"], a["L3_ffn_e_score_correction_bias"]])
    d["rows"] = np.ascontiguousarray(np.broadcast_to(row, (P, NROW)))
    return {n: np.ascontiguousarray(v) for n, v in d.items()}


def kernel(**inputs):
    import numpy as np
    import concourse.bacc as bacc
    from concourse.bass_utils import run_bass_kernel_spmd

    nc = bacc.Bacc("TRN2", target_bir_lowering=False, num_devices=1)
    arrays = {f"in_{n}": v for n, v in layout(inputs).items()}
    dram = {n[3:]: nc.dram_tensor(n, v.shape, mybir.dt.from_np(v.dtype), kind="ExternalInput").ap()
            for n, v in arrays.items()}
    out = nc.dram_tensor("out", (P, T), F32, kind="ExternalOutput").ap()
    build(nc, dram, out)
    r = run_bass_kernel_spmd(nc, [arrays], core_ids=[0])
    got = np.asarray(r.results[0]["out"])
    return np.ascontiguousarray(got.reshape(P, NB, P).transpose(1, 0, 2))
```
